# Optimizing a Trainium2 kernel written in Bass

```python
import numpy as np
import jax
import jax.numpy as jnp

def _softmax(x, axis=-1):
    return jax.nn.softmax(x, axis=axis)

def _gelu(x):
    return jax.nn.gelu(x, approximate=True)

def _silu(x):
    return jax.nn.silu(x)

def _sigmoid(x):
    return jax.nn.sigmoid(x)

def _layernorm(x, axis=-1, eps=1e-05):
    m = jnp.mean(x, axis=axis, keepdims=True)
    v = jnp.var(x, axis=axis, keepdims=True)
    return (x - m) / jnp.sqrt(v + eps)

def _scatter_add(tgt, idx, src, axis=0):
    return tgt.at[idx].add(src)

def _segment_sum(src, seg, n):
    return jax.ops.segment_sum(src, seg, n)
kernel_name = 'mk_adj_resnorm_d4_adj_r2_6883af'

def setup_inputs(seed: int=0):
    np.random.seed(seed)
    _w = jnp.asarray

    def _rec_inputs():
        import jax
        import jax.numpy as jnp
        _gk = jax.random.key(seed)
        x = -0.000929 + 1 * jax.random.normal(jax.random.fold_in(_gk, 1), (4096, 128), jnp.float32)
        _a = jax.random.bernoulli(jax.random.fold_in(_gk, 2), 0.00195312, (4096, 4096))
        _af = _a.astype(jnp.float32)
        adj = _af
        return (x, adj)
    x, adj = _rec_inputs()

    def _L0_gnn_setup():
        import jax, jax.numpy as jnp
        import numpy as np
        N, EMB, HID = (4096, 128, 128)
        key = jax.random.key(seed)
        k1, k2, k3, k4, k5, k6, k7, k8 = jax.random.split(key, 8)
        inlayer = jax.random.normal(k1, (N, EMB), dtype=jnp.float32)
        inlayer2 = jax.random.normal(k2, (N, 2 * EMB), dtype=jnp.float32)
        adj_mat = jax.random.randint(k3, (N, N), 0, 2).astype(jnp.float32)
        W1 = jax.random.normal(k4, (HID, 2 * EMB), dtype=jnp.float32) / np.sqrt(2 * EMB)
        w2 = jax.random.normal(k5, (HID,), dtype=jnp.float32) / np.sqrt(HID)
        b2 = jax.random.normal(k6, (), dtype=jnp.float32) * 0.01
        w3 = jax.random.normal(k7, (HID,), dtype=jnp.float32) / np.sqrt(HID)
        b3 = jax.random.normal(k8, (), dtype=jnp.float32) * 0.01
        return {'inlayer': inlayer, 'inlayer2': inlayer2, 'adj_mat': adj_mat, 'W1': W1, 'w2': w2, 'b2': b2, 'w3': w3, 'b3': b3}
    _L0_gnn_all = _L0_gnn_setup()
    _L0_gnn_in = {k: v for k, v in _L0_gnn_all.items() if k in ('inlayer2', 'W1', 'w2', 'b2', 'w3', 'b3')}
    del _L0_gnn_all

    def _L1_gnn_setup():
        import jax, jax.numpy as jnp
        import numpy as np
        N = 4096
        H = 128
        key = jax.random.key(seed)
        k_x, k_A, k_W = jax.random.split(key, 3)
        x = jax.random.normal(k_x, (N, H), dtype=jnp.float32)
        A = jax.random.uniform(k_A, (N, N), dtype=jnp.float32)
        alpha = jnp.array([0.5], dtype=jnp.float32)
        bound = 1.0 / np.sqrt(H)
        W = jax.random.uniform(k_W, (H, H), dtype=jnp.float32, minval=-bound, maxval=bound)
        b = jnp.zeros((H,), dtype=jnp.float32)
        t = jnp.zeros((1,), dtype=jnp.float32)
        return {'t': t, 'x': x, 'A': A, 'alpha': alpha, 'W': W, 'b': b}
    _L1_gnn_all = _L1_gnn_setup()
    _L1_gnn_in = {k: v for k, v in _L1_gnn_all.items() if k in ('t', 'alpha', 'W', 'b')}
    del _L1_gnn_all

    def _L2_gnn_setup():
        import jax, jax.numpy as jnp
        import numpy as np
        K = 5
        TAU = 0.5
        N = 4096
        IN_DIM = 128
        OUT_DIM = 128

        def _cheb_coeff(k_order: int, tau: float) -> jnp.ndarray:
            ks = jnp.arange(k_order, dtype=jnp.float32)
            x_k = jnp.cos(jnp.pi * (ks + 0.5) / k_order)
            return 2.0 / k_order * jnp.exp(-tau * x_k)
        key = jax.random.key(seed)
        k1, k2, k3 = jax.random.split(key, 3)
        x = jax.random.normal(k1, (N, IN_DIM), dtype=jnp.float32)
        laplacian = jax.random.normal(k2, (N, N), dtype=jnp.float32) / np.sqrt(N)
        limit = np.sqrt(6.0 / (IN_DIM + OUT_DIM))
        theta = jax.random.uniform(k3, (K, IN_DIM, OUT_DIM), dtype=jnp.float32, minval=-limit, maxval=limit)
        return {'x': x, 'laplacian': laplacian, 'theta': theta}
    _L2_gnn_all = _L2_gnn_setup()
    _L2_gnn_in = {k: v for k, v in _L2_gnn_all.items() if k in ('theta',)}
    del _L2_gnn_all

    def _L3_gnn_setup():
        import jax, jax.numpy as jnp
        import numpy as np
        N = 8192
        D = 128
        key = jax.random.key(seed)
        k1, k2 = jax.random.split(key)
        features = jax.random.normal(k1, (N, D), dtype=jnp.float32)
        adj = jax.random.uniform(k2, (N, N), dtype=jnp.float32)
        return {'features': features, 'adj': adj}
    _L3_gnn_all = _L3_gnn_setup()
    _L3_gnn_in = {k: v for k, v in _L3_gnn_all.items() if k in ()}
    del _L3_gnn_all
    return {'x': x, 'adj': adj, 'L0_gnn_inlayer2': _L0_gnn_in['inlayer2'], 'L0_gnn_W1': _L0_gnn_in['W1'], 'L0_gnn_w2': _L0_gnn_in['w2'], 'L0_gnn_b2': _L0_gnn_in['b2'], 'L0_gnn_w3': _L0_gnn_in['w3'], 'L0_gnn_b3': _L0_gnn_in['b3'], 'L1_gnn_t': _L1_gnn_in['t'], 'L1_gnn_alpha': _L1_gnn_in['alpha'], 'L1_gnn_W': _L1_gnn_in['W'], 'L1_gnn_b': _L1_gnn_in['b'], 'L2_gnn_theta': _L2_gnn_in['theta']}

def reference(x, adj, L0_gnn_inlayer2, L0_gnn_W1, L0_gnn_w2, L0_gnn_b2, L0_gnn_w3, L0_gnn_b3, L1_gnn_t, L1_gnn_alpha, L1_gnn_W, L1_gnn_b, L2_gnn_theta):
    import jax
    import jax.numpy as jnp

    def _L0_gnn_ref(inlayer, inlayer2, adj_mat, W1, w2, b2, w3, b3):
        import jax, jax.numpy as jnp
        import numpy as np
        N, EMB, HID = (4096, 128, 128)
        in_fts = jnp.einsum('ne,he->nh', inlayer2, W1)
        f1 = in_fts @ w2 + b2
        f2 = in_fts @ w3 + b3
        logits = f1[:, None] + f2[None, :]
        logits = adj_mat * logits
        bias_mat = -1000000000.0 * (1.0 - (adj_mat > 0).astype(jnp.float32))
        coefs = jax.nn.softmax(jax.nn.leaky_relu(logits, 0.01) + bias_mat, axis=1)
        vals = coefs @ inlayer
        return vals

    def _L1_gnn_ref(t, x, A, alpha, W, b):
        import jax, jax.numpy as jnp
        import numpy as np
        N = 4096
        H = 128
        a = alpha[0]
        A_prime = a * A
        diag = jnp.diagonal(A_prime) + (1.0 - a)
        A_prime = A_prime.at[jnp.arange(N), jnp.arange(N)].set(diag)
        out_degree = A_prime.sum(axis=1)
        inv_deg = jnp.where(out_degree == 0.0, 0.0, 1.0 / out_degree)
        x = inv_deg[:, None] * A_prime @ x
        x = x @ W.T + b
        return jax.nn.relu(x)

    def _L2_gnn_ref(x, laplacian, theta):
        import jax, jax.numpy as jnp
        import numpy as np
        K = 5
        TAU = 0.5
        N = 4096
        IN_DIM = 128
        OUT_DIM = 128

        def _cheb_coeff(k_order: int, tau: float) -> jnp.ndarray:
            ks = jnp.arange(k_order, dtype=jnp.float32)
            x_k = jnp.cos(jnp.pi * (ks + 0.5) / k_order)
            return 2.0 / k_order * jnp.exp(-tau * x_k)
        coeff = _cheb_coeff(K, TAU)
        tx_prev, tx_curr = (x, laplacian @ x)
        tx_list = [tx_prev, tx_curr]
        for _ in range(2, K):
            tx_next = 2.0 * (laplacian @ tx_curr) - tx_prev
            tx_list.append(tx_next)
            tx_prev, tx_curr = (tx_curr, tx_next)
        tx_stack = jnp.stack(tx_list, axis=0)
        return jnp.einsum('kni,kio,k->no', tx_stack, theta, coeff)

    def _L3_gnn_ref(features, adj):
        import jax, jax.numpy as jnp
        import numpy as np
        N = 8192
        D = 128
        return jnp.matmul(adj, features)
    x = _layernorm(x + _L0_gnn_ref(x, L0_gnn_inlayer2, adj, L0_gnn_W1, L0_gnn_w2, L0_gnn_b2, L0_gnn_w3, L0_gnn_b3), axis=-1)
    x = _layernorm(x + _L1_gnn_ref(L1_gnn_t, x, adj, L1_gnn_alpha, L1_gnn_W, L1_gnn_b), axis=-1)
    x = _layernorm(x + _L2_gnn_ref(x, adj, L2_gnn_theta), axis=-1)
    x = _layernorm(x + _L3_gnn_ref(x, adj), axis=-1)
    return x

_drawn_inputs = setup_inputs


def setup_inputs(seed=0):
    import zlib

    import numpy as np

    out = dict(_drawn_inputs(seed))
    spreads = {'L1_gnn_b': (0.0, 0.1)}
    factors = {}
    for name, (base, spread) in spreads.items():
        noise = np.random.default_rng([zlib.crc32(name.encode()), seed]).standard_normal(out[name].shape)
        drawn = base * np.exp(spread * noise) if base else spread * noise
        out[name] = jnp.asarray(drawn.astype(out[name].dtype))
    for name, factor in factors.items():
        out[name] = (out[name] * factor).astype(out[name].dtype)
    return out
```

```python
from contextlib import ExitStack

import numpy as np

import concourse.bass as bass
from concourse import mybir


def gnn_kernel(nc, adj_blocks, x_nodes, in2_t, w1, w23, wt, theta, row_params, out):
    fp32 = mybir.dt.float32
    fp16 = mybir.dt.float16
    fp8 = mybir.dt.float8e4
    i32 = mybir.dt.int32
    ALU = mybir.AluOpType
    ACT = mybir.ActivationFunctionType
    AX = mybir.AxisListType
    RMAX = bass.bass_isa.ReduceOp.max

    N = 4096
    D = 128
    P = 128
    T = N // P
    ORDERS = theta.shape[1]
    EPS = 1e-5
    SLOPE = 0.01
    TAU = 0.5
    COEFF = [2.0 / ORDERS * float(np.exp(-TAU * np.cos(np.pi * (k + 0.5) / ORDERS))) for k in range(ORDERS)]
    EXPONENT_BITS = 0x7F800000
    PART_TOP = 2.0 ** 15
    TINY = 1e-30

    PAIRS = 8
    LOGIT_LIMIT = 32.0
    LOW_LIMIT = 4000.0

    SPAN = 1024
    SPANS = N // SPAN
    SPAN_TILES = SPAN // P
    LOAD_TILES = 2
    LOADS = SPANS * T // LOAD_TILES
    LOADS_PER_SPAN = T // LOAD_TILES
    DX = D + 1
    PER_BANK = 3
    SPAN_BANKS = -(-SPAN_TILES // PER_BANK)
    QUAD = 4
    QUADS = T // QUAD
    WIDE = QUAD * D
    GW = 2 * D + 1

    with ExitStack() as ctx:
        def sb(name, shape, dt=fp32):
            return ctx.enter_context(nc.sbuf_tensor(name, shape, dt))

        def sem(name):
            return ctx.enter_context(nc.semaphore(name))

        adj8 = sb("adj8", [P, T * N], fp8)
        adj3 = adj8[:, :].rearrange("p (t n) -> p t n", t=T)
        in2 = adj8[:, (T - 8) * N:].bitcast(fp32).rearrange("p (e n) -> p e n", e=2)
        xh = sb("xh", [P, T * DX])
        x3 = xh[:, :].rearrange("p (t d) -> p t d", t=T)
        h2t = xh[:, 0:N]
        h = sb("h", [P, N])
        h3d = h[:, :].rearrange("p (t d) -> p t d", t=T)
        work = sb("work", [P, 8208])
        stage = work[:, 0:2 * LOAD_TILES * SPAN].rearrange("p (s t n) -> p s t n", s=2, t=LOAD_TILES)
        expo = work[:, 4096:4096 + 2 * SPAN].rearrange("p (s n) -> p s n", s=2)
        weight = work[:, 6144:6144 + 2 * SPAN].rearrange("p (s n) -> p s n", s=2)
        gparts = work[:, 0:T * GW // 2].bitcast(fp16).rearrange("p (t w) -> p t w", t=T)
        g_own = work[:, 4112:4112 + N].rearrange("p (t d) -> p t d", t=T)
        parts = [work[:, base:base + N].bitcast(fp16).rearrange("p (m q w) -> p m q w", m=QUADS, q=2)
                 for base in (0, 4112)]
        tmp = sb("tmp", [P, 1536])
        xr = tmp[:, 0:SPAN_TILES * D].rearrange("p (t d) -> p t d", t=SPAN_TILES)
        mix = tmp[:, 1024:1024 + D]
        v_cols = tmp[:, 0:4]
        v1_wide = tmp[:, 512:512 + 2 * P].rearrange("p (e n) -> p e n", e=2)
        w2_wide = tmp[:, 1024:1024 + P]
        squares = tmp[:, 0:(ORDERS + 1) * D]
        w1_sb = sb("w1_sb", [P, 2 * P])
        w23_sb = sb("w23_sb", [P, 2])
        wt_sb = sb("wt_sb", [P, D])
        th = sb("th", [P, ORDERS * D])
        th_scaled = sb("th_scaled", [P, (ORDERS - 1) * D])
        rows = sb("rows", [P, 3 + D])
        b2_col, b3_col, alpha_col, bias_row = rows[:, 0:1], rows[:, 1:2], rows[:, 2:3], rows[:, 3:3 + D]
        ident = sb("ident", [P, P])
        ones = sb("ones", [P, P])
        xsum = sb("xsum", [P, D])
        f1_cols = sb("f1_cols", [P, T])
        f2_cols = sb("f2_cols", [P, T])
        q_cols = sb("q_cols", [P, T])
        low_cols = sb("low_cols", [P, T])
        eps_col = sb("eps_col", [P, 1])
        isolated = sb("isolated", [P, SPAN_TILES])
        denom = sb("denom", [P, SPAN_TILES])
        inv_denom = sb("inv_denom", [P, SPAN_TILES])
        stats = sb("stats", [P, 6 * 2])
        mv = sb("mv", [P, 2 * SPAN_TILES])
        mv3 = mv[:, :].rearrange("p (t k) -> p t k", k=2)
        std = sb("std", [P, SPAN_TILES])
        rstd = sb("rstd", [P, SPAN_TILES])
        deg = sb("deg", [P, T])
        limits = sb("limits", [P, 8])
        flag = sb("flag", [P, 1], i32)
        lift_cols = sb("lift_cols", [P, T])
        diag = work[:, 4096:4096 + SPAN].rearrange("p (t n) -> p t n", t=SPAN_TILES)
        run_max = work[:, 4096:4096 + SPAN]
        row_max = work[:, 5120:5120 + SPAN]
        exp_up, exp_low = run_max, row_max
        careful_weight = work[:, 6144:6144 + SPAN]
        up_row = work[:, 7168:7168 + SPAN]
        small = sb("small", [P, 16])
        scales = sb("scales", [P, 16])
        S_G, INV_SG, ONE_MINUS_A, S4, GROW, INV_GROW = [scales[:, n:n + 1] for n in range(6)]
        OWN = scales[:, 13:14]
        EV, SUB, EV0, SUB0 = [scales[:, n:n + 1] for n in range(6, 10)]
        S_K = {4: S4, 3: scales[:, 10:11], 2: scales[:, 11:12], 1: scales[:, 12:13]}

        bank = [ctx.enter_context(nc.psum_tensor(f"bank{n}", [P, WIDE], fp32)) for n in range(8)]

        weights_in = [sem(f"weights_in{n}") for n in range(6)]
        in2_in = [sem("in2_in0"), sem("in2_in1")]
        x_in = sem("x_in")
        stage_in = [sem("stage_in0"), sem("stage_in1")]
        xr_in = sem("xr_in")
        out_stored = [sem("out_stored0"), sem("out_stored1")]
        const_ready = sem("const_ready")
        pool_reduced = sem("pool_reduced")
        act_step = sem("act_step")
        dve_step = sem("dve_step")
        w2_wide_ready = sem("w2_wide_ready")
        v_done = sem("v_done")
        v_ready = sem("v_ready")
        f_cols_done = sem("f_cols_done")
        f_cols_ready = sem("f_cols_ready")
        f1_row_done = sem("f1_row_done")
        f1_row_ready = sem("f1_row_ready")
        squares_ready = sem("squares_ready")
        norms_done = sem("norms_done")
        part_scale_var = sem("part_scale_var")
        part_scale_root = sem("part_scale_root")
        part_scales_ready = sem("part_scales_ready")
        xsum_done = sem("xsum_done")
        q_ready = sem("q_ready")
        limits_ready = sem("limits_ready")
        limits_reduced = sem("limits_reduced")
        flag_ready = sem("flag_ready")
        careful_x_in = sem("careful_x_in")
        careful_in = [sem("careful_in0"), sem("careful_in1")]
        careful_used = [sem("careful_used0"), sem("careful_used1")]
        careful_step = sem("careful_step")
        diag_ready = sem("diag_ready")
        f1_spread = sem("f1_spread")
        row_max_ready = sem("row_max_ready")
        rows_ready = sem("rows_ready")
        exps_ready = sem("exps_ready")
        careful_ready = sem("careful_ready")
        careful_multiplied = sem("careful_multiplied")
        careful_var = sem("careful_var")
        careful_std = sem("careful_std")
        careful_done = sem("careful_done")
        careful_zeroed = sem("careful_zeroed")
        cast_by_act = sem("cast_by_act")
        cast_by_dve = sem("cast_by_dve")
        expo_ready = sem("expo_ready")
        weight_ready = sem("weight_ready")
        weight_used = sem("weight_used")
        var_ready = sem("var_ready")
        std_ready = sem("std_ready")
        h1_ready = sem("h1_ready")
        turn_done = sem("turn_done")
        turn_copied = sem("turn_copied")
        g_done = sem("g_done")
        g_copied = sem("g_copied")
        g_low_ready = sem("g_low_ready")
        diff_done = sem("diff_done")
        diff_low = sem("diff_low")
        diff_read = sem("diff_read")
        var1_ready = sem("var1_ready")
        std1_ready = sem("std1_ready")
        h2_ready = sem("h2_ready")
        h2t_done = sem("h2t_done")
        h2t_copied = sem("h2t_copied")
        b4_done = sem("b4_done")
        parts_ready = sem("parts_ready")
        deg_max = sem("deg_max")
        theta_ready = sem("theta_ready")
        acc_done = sem("acc_done")
        acc_copied = sem("acc_copied")
        back_done = sem("back_done")
        back_read = sem("back_read")
        var2_ready = sem("var2_ready")
        std2_ready = sem("std2_ready")
        out_ready = sem("out_ready")

        block = ctx.enter_context(nc.Block())

        def on_dve(load):
            return load % 8 in (2, 5, 7)

        def casts(load, dve):
            return sum(on_dve(m) == dve for m in range(load + 1))

        def wait_cast(eng, load):
            eng.wait_ge(cast_by_dve if on_dve(load) else cast_by_act, casts(load, on_dve(load)))

        def load_of(load):
            return load // LOADS_PER_SPAN, load % LOADS_PER_SPAN * LOAD_TILES

        def cast_target(load):
            c, j = load_of(load)
            return adj3[:, j:j + LOAD_TILES, c * SPAN:(c + 1) * SPAN]

        def att_acc(c, t, cols=slice(0, DX)):
            b = SPAN_BANKS * (c % 2) + t // PER_BANK
            base = t % PER_BANK * DX
            return bank[b][:, base + cols.start:base + cols.stop]

        STD_AT = 20

        def turned_slot(c):
            return h[:, c % 2 * WIDE:(c % 2 + 1) * WIDE]

        def out_slot(c):
            return h[:, (2 + c % 2) * WIDE:(3 + c % 2) * WIDE]

        old_b = h[:, 4 * WIDE:5 * WIDE]
        new_b = h[:, 5 * WIDE:6 * WIDE]

        @block.sync
        def _(sp):
            for e in range(2):
                sp.dma_start(in2[:, e, :], in2_t[:, e, :]).then_inc(in2_in[e], 16)

            def load_residual(c):
                if c >= 1:
                    sp.wait_ge(h1_ready, SPAN_TILES * c)
                sp.dma_start(xr, x_nodes[:, c * SPAN_TILES:(c + 1) * SPAN_TILES, :]).then_inc(xr_in, 16)

            for load in range(LOADS):
                c, _j = load_of(load)
                if load >= 2:
                    wait_cast(sp, load - 2)
                sp.dma_start(stage[:, load % 2, :, :], adj_blocks[c, load % LOADS_PER_SPAN, :, :, :])\
                    .then_inc(stage_in[load % 2], 16)
                if load == 1:
                    sp.dma_start(x3[:, :, 0:D], x_nodes).then_inc(x_in, 16)
                if c >= 1 and load % LOADS_PER_SPAN == 1:
                    load_residual(c - 1)
            load_residual(SPANS - 1)

            sp.wait_ge(flag_ready, 1)
            with sp.If(sp.value_load(flag[0:1, 0:1], min_val=0, max_val=1)):
                sp.wait_ge(h1_ready, T)
                for c in range(SPANS):
                    if c >= 1:
                        sp.wait_ge(careful_done, c)
                    sp.dma_start(xr, x_nodes[:, bass.ds(c * SPAN_TILES, SPAN_TILES), :]).then_inc(careful_x_in, 16)
                    for sweep in range(2):
                        if sweep == 1:
                            for s in range(2):
                                sp.wait_ge(careful_used[s], (c + 1) * PAIRS + 1)
                        with sp.Fori(0, PAIRS) as pair:
                            for s in range(2):
                                source = sp.snap(pair * 2 + s)
                                if sweep == 0:
                                    sp.wait_ge(careful_used[s], c * PAIRS + pair + 1)
                                else:
                                    sp.wait_ge(careful_ready, c * T + pair * 2 * LOAD_TILES + 1)
                                sp.dma_start(stage[:, s, :, :], adj_blocks[c, source, :, :, :])\
                                    .then_inc(careful_in[s], 16)
            out_tiles = out.rearrange("(t p) d -> p t d", p=P)
            for c in range(QUADS):
                sp.wait_ge(out_ready, c + 1)
                sp.dma_start(out_tiles[:, c * QUAD:(c + 1) * QUAD, :],
                             out_slot(c).rearrange("p (t d) -> p t d", t=QUAD)).then_inc(out_stored[c % 2], 16)
            for s in range(2):
                sp.wait_ge(out_stored[s], 16 * QUADS // 2)

        @block.gpsimd
        def _(pool):
            nc.gpsimd.memset(ones[:, :], 1.0).then_inc(const_ready, 1)
            nc.gpsimd.memset(eps_col[:, :], EPS).then_inc(const_ready, 1)
            nc.gpsimd.memset(ident[:, :], 0.0).then_inc(const_ready, 1)
            pool.wait_ge(const_ready, 3)
            nc.gpsimd.affine_select(out=ident[:, :], in_=ident[:, :], compare_op=ALU.not_equal, fill=1.0,
                                    base=0, pattern=[[-1, P]], channel_multiplier=1).then_inc(const_ready, 1)
            nc.gpsimd.memset(x3[:, :, D:DX], 1.0).then_inc(const_ready, 1)
            pool.wait_ge(limits_ready, 1)
            nc.gpsimd.partition_all_reduce(limits[:, 4:6], limits[:, 2:4], P, RMAX).then_inc(limits_reduced, 1)
            pool.wait_ge(flag_ready, 1)
            with pool.If(pool.value_load(flag[0:1, 0:1], min_val=0, max_val=1)):
                for c in range(SPANS):
                    pool.wait_ge(careful_used[1], (c + 1) * PAIRS + 1)
                    nc.gpsimd.partition_all_reduce(row_max, run_max, P, RMAX).then_inc(row_max_ready, 1)
            pool.wait_ge(deg_max, 1)
            nc.gpsimd.partition_all_reduce(small[:, 9:10], small[:, 8:9], P, RMAX).then_inc(pool_reduced, 1)

        @block.scalar
        def _(act):
            for n, (dst, src) in enumerate(((w1_sb, w1), (w23_sb, w23), (rows, row_params), (wt_sb, wt))):
                act.dma_start(dst[:, :], src).then_inc(weights_in[n], 16)
            act.dma_start(th[:, :], theta.rearrange("p k d -> p (k d)")).then_inc(weights_in[4], 16)

            act.wait_ge(v_done, 1)
            nc.scalar.copy(v_cols, bank[6][:, 0:4]).then_inc(v_ready, 1)
            act.wait_ge(v_done, 2)
            nc.scalar.copy(v1_wide, bank[7][:, 0:2 * P].rearrange("p (e n) -> p e n", e=2)).then_inc(v_ready, 1)
            act.wait_ge(weights_in[2], 16)
            for c in range(QUADS):
                act.wait_ge(f1_row_done, c + 1)
                nc.scalar.activation(h[:, c * WIDE:(c + 1) * WIDE], bank[c % 4][:, :], ACT.Identity,
                                     bias=b2_col).then_inc(f1_row_ready, 1)
            act.wait_ge(part_scale_var, 1)
            nc.scalar.activation(small[:, 4:6], small[:, 2:4], ACT.Sqrt).then_inc(part_scale_root, 1)
            act.wait_ge(f_cols_ready, 1)
            act.wait_ge(f_cols_ready, 2)
            nc.scalar.activation(q_cols[:, :], f2_cols[:, :], ACT.Exp, scale=SLOPE).then_inc(q_ready, 1)

            act.wait_ge(f1_row_ready, QUADS)
            for c in range(SPANS):
                for j in range(T):
                    n = c * T + j
                    if j % LOAD_TILES == 0:
                        load = n // LOAD_TILES
                        if not on_dve(load):
                            if c == 0 and j == T - 8:
                                act.wait_ge(f_cols_done, 1)
                            act.wait_ge(stage_in[load % 2], 16 * (load // 2 + 1))
                            nc.scalar.activation(cast_target(load), stage[:, load % 2, :, :], ACT.Copy,
                                                 saturate=False).then_inc(cast_by_act, 1)
                    if n >= 2:
                        act.wait_ge(weight_ready, n - 1)
                    nc.scalar.activation(expo[:, n % 2, :], h[:, c * SPAN:(c + 1) * SPAN], ACT.Exp,
                                         bias=f2_cols[:, j:j + 1], scale=1.0 - SLOPE).then_inc(expo_ready, 1)
                    if c >= 1 and j == STD_AT:
                        act.wait_ge(var_ready, c)
                        nc.scalar.activation(std[:, :], mv3[:, :, 1], ACT.Sqrt, bias=eps_col[:, :])\
                            .then_inc(std_ready, 1)
            act.wait_ge(var_ready, SPANS)
            nc.scalar.activation(std[:, :], mv3[:, :, 1], ACT.Sqrt, bias=eps_col[:, :]).then_inc(std_ready, 1)

            act.wait_ge(flag_ready, 1)
            with act.If(act.value_load(flag[0:1, 0:1], min_val=0, max_val=1)):
                for c in range(SPANS):
                    act.wait_ge(rows_ready, c + 1)
                    with act.Fori(0, T) as j:
                        act.wait_ge(careful_ready, c * T + j + 1)
                        nc.scalar.activation(exp_up, up_row, ACT.Exp, bias=f2_cols[:, bass.ds(j, 1)])
                        nc.scalar.activation(exp_low, h[:, bass.ds(c * SPAN, SPAN)], ACT.Exp,
                                             bias=low_cols[:, bass.ds(j, 1)]).then_inc(exps_ready, 1)
                    act.wait_ge(careful_var, c + 1)
                    nc.scalar.activation(std[:, :], mv3[:, :, 1], ACT.Sqrt, bias=eps_col[:, :])\
                        .then_inc(careful_std, 1)

            for m in range(QUADS):
                act.wait_ge(turn_done, m + 1)
                if m >= 2:
                    act.wait_ge(g_done, m - 1)
                nc.scalar.copy(tmp[:, m % 2 * WIDE:(m % 2 + 1) * WIDE], bank[m % 2][:, :])\
                    .then_inc(turn_copied, 1)
                act.wait_ge(g_done, m + 1)
                nc.scalar.mul(g_own[:, m * QUAD:(m + 1) * QUAD, :], bank[4 + m % 2][:, :]
                              .rearrange("p (t d) -> p t d", t=QUAD), OWN).then_inc(g_copied, 1)

            for t in range(T + 3):
                if t < T:
                    act.wait_ge(diff_done, t + 1)
                    if t >= 2:
                        act.wait_ge(diff_read, t - 1)
                    nc.scalar.copy(tmp[:, t % 2 * DX:(t % 2 + 1) * DX], bank[t % 4][:, D:GW]).then_inc(diff_low, 1)
                if 1 <= t <= T:
                    act.wait_ge(var1_ready, t)
                    nc.scalar.activation(std[:, (t - 1) % 2:(t - 1) % 2 + 1], mv3[:, (t - 1) % 2, 1:2], ACT.Sqrt,
                                         bias=eps_col[:, :]).then_inc(std1_ready, 1)
                if t >= 6 and t % QUAD == 2:
                    m = t // QUAD - 1
                    act.wait_ge(h2t_done, m + 1)
                    nc.scalar.copy(h2t[:, m * WIDE:(m + 1) * WIDE], bank[4 + m % 2][:, :]).then_inc(h2t_copied, 1)

            act.wait_ge(theta_ready, 1)
            for q in range(ORDERS):
                k = ORDERS - 2 - q
                for c in range(QUADS):
                    n = q * QUADS + c
                    act.wait_ge(acc_done, n + 1)
                    if n >= 2:
                        act.wait_ge(back_done, n - 1)
                    scale = EV if k >= 1 else EV0 if k == 0 else 1.0
                    nc.scalar.mul(turned_slot(n), bank[n % 2][:, :], scale).then_inc(acc_copied, 1)
                    if k <= 0:
                        r = (q - ORDERS + 2) * QUADS + c
                        act.wait_ge(var2_ready, r + 1)
                        nc.scalar.activation(std[:, 0:QUAD], mv3[:, 0:QUAD, 1], ACT.Sqrt, bias=eps_col[:, :])\
                            .then_inc(std2_ready, 1)

        @block.vector
        def _(dve):
            steps = [0]

            def step(ins):
                steps[0] += 1
                ins.then_inc(dve_step, 1)
                dve.wait_ge(dve_step, steps[0])

            tt, ts, stt = nc.vector.tensor_tensor, nc.vector.tensor_scalar, nc.vector.scalar_tensor_tensor
            dve.wait_ge(const_ready, 5)
            dve.wait_ge(weights_in[1], 16)
            ts(w2_wide, ones[:, :], w23_sb[:, 0:1], None, ALU.mult).then_inc(w2_wide_ready, 1)
            dve.wait_ge(weights_in[2], 16)
            dve.wait_ge(f_cols_done, 1)
            f_psum = bank[6][:, 64:64 + 2 * T].rearrange("p (t k) -> p t k", k=2)
            ts(f1_cols[:, :], f_psum[:, :, 0], b2_col, None, ALU.add).then_inc(f_cols_ready, 1)
            ts(f2_cols[:, :], f_psum[:, :, 1], b3_col, None, ALU.add).then_inc(f_cols_ready, 1)

            dve.wait_ge(f_cols_ready, 2)
            step(nc.vector.reduce_max(limits[:, 0:1], f1_cols[:, :], AX.X))
            step(nc.vector.reduce_max(limits[:, 1:2], f2_cols[:, :], AX.X))
            step(ts(low_cols[:, :], f2_cols[:, :], -1.0, None, ALU.mult))
            step(nc.vector.reduce_max(limits[:, 3:4], low_cols[:, :], AX.X))
            step(tt(limits[:, 0:1], limits[:, 0:1], limits[:, 1:2], ALU.max))
            stt(limits[:, 2:3], limits[:, 3:4], LOGIT_LIMIT / LOW_LIMIT, limits[:, 0:1], ALU.mult, ALU.max)\
                .then_inc(limits_ready, 1)
            dve.wait_ge(limits_reduced, 1)
            step(ts(low_cols[:, :], f2_cols[:, :], SLOPE, None, ALU.mult))
            ts(flag[:, :], limits[:, 4:5], LOGIT_LIMIT, None, ALU.is_gt).then_inc(flag_ready, 1)

            dve.wait_ge(weights_in[3], 16)
            dve.wait_ge(weights_in[4], 16)
            dve.wait_ge(f1_row_done, QUADS)
            dve.wait_ge(v_ready, 2)
            step(tt(squares[:, 0:D], wt_sb[:, :], wt_sb[:, :], ALU.mult))
            for k in range(ORDERS):
                step(ts(th[:, k * D:(k + 1) * D], th[:, k * D:(k + 1) * D], COEFF[k], None, ALU.mult))
            tt(squares[:, D:], th[:, :], th[:, :], ALU.mult).then_inc(squares_ready, 1)
            dve.wait_ge(norms_done, 1)
            step(nc.vector.reduce_max(small[:, 0:1], bank[5][:, 0:D], AX.X))
            step(nc.vector.reduce_max(small[:, 6:7], bank[5][:, D:WIDE], AX.X))
            step(nc.vector.reduce_max(small[:, 7:8], bank[4][:, 0:2 * D], AX.X))
            step(tt(small[:, 1:2], small[:, 6:7], small[:, 7:8], ALU.max))
            step(ts(small[:, 0:2], small[:, 0:2], D / PART_TOP ** 2, TINY, ALU.mult, ALU.max))
            nc.vector.reciprocal(small[:, 2:4], small[:, 0:2]).then_inc(part_scale_var, 1)
            dve.wait_ge(part_scale_root, 1)
            step(ts(small[:, 10:12].bitcast(i32), small[:, 4:6].bitcast(i32), EXPONENT_BITS, None, ALU.bitwise_and))
            step(nc.vector.tensor_copy(S_G, small[:, 10:11]))
            step(nc.vector.tensor_copy(S4, small[:, 11:12]))
            step(nc.vector.reciprocal(INV_SG, S_G))
            step(ts(ONE_MINUS_A, alpha_col, -1.0, 1.0, ALU.mult, ALU.add))
            step(tt(OWN, ONE_MINUS_A, S_G, ALU.mult))
            dve.wait_ge(xsum_done, 1)
            step(nc.vector.tensor_copy(xsum[:, :], bank[7][:, 0:D]))
            step(ts(th[:, (ORDERS - 1) * D:], th[:, (ORDERS - 1) * D:], S4, None, ALU.mult))

            def att_scalars(c, step=step):
                for b in range(SPAN_BANKS):
                    k = min(PER_BANK, SPAN_TILES - b * PER_BANK)
                    sums = bank[SPAN_BANKS * (c % 2) + b][:, 0:k * DX].rearrange("p (t w) -> p t w", w=DX)[:, :, D]
                    cols = slice(b * PER_BANK, b * PER_BANK + k)
                    step(ts(isolated[:, cols], sums, 0.0, None, ALU.is_equal))
                    step(stt(denom[:, cols], isolated[:, cols], float(N), sums, ALU.mult, ALU.add))
                step(nc.vector.reciprocal(inv_denom[:, :], denom[:, :]))

            def att_tile(c, t):
                if t == 0:
                    dve.wait_ge(xr_in, 16 * (c + 1))
                step(stt(mix, xsum[:, :], isolated[:, t:t + 1], att_acc(c, t, slice(0, D)), ALU.mult, ALU.add))
                step(stt(xr[:, t, :], mix, inv_denom[:, t:t + 1], xr[:, t, :], ALU.mult, ALU.add))
                step(nc.vector.bn_stats(stats[:, 0:6], xr[:, t, :]))
                last = nc.vector.bn_aggr(mv3[:, t, :], stats[:, 0:6])
                if t == SPAN_TILES - 1:
                    last.then_inc(var_ready, 1)
                    dve.wait_ge(var_ready, c + 1)
                else:
                    step(last)

            def att_rstd(c):
                dve.wait_ge(std_ready, c + 1)
                step(nc.vector.reciprocal(rstd[:, :], std[:, :]))

            def att_norm(c, t):
                ts(h3d[:, c * SPAN_TILES + t, :], xr[:, t, :], mv3[:, t, 0:1], rstd[:, t:t + 1],
                   ALU.subtract, ALU.mult).then_inc(h1_ready, 1)

            dve.wait_ge(q_ready, 1)
            for c in range(SPANS):
                for j in range(T):
                    n = c * T + j
                    load = n // LOAD_TILES
                    if j % LOAD_TILES == 0 and on_dve(load):
                        if c == 0 and j == T - 8:
                            pass
                        dve.wait_ge(stage_in[load % 2], 16 * (load // 2 + 1))
                        nc.vector.tensor_copy(cast_target(load), stage[:, load % 2, :, :], saturate=False)\
                            .then_inc(cast_by_dve, 1)
                    wait_cast(dve, load)
                    dve.wait_ge(expo_ready, n + 1)
                    if n >= 2:
                        dve.wait_ge(weight_used, n - 1)
                    stt(weight[:, n % 2, :], expo[:, n % 2, :], q_cols[:, j:j + 1],
                        adj3[:, j, c * SPAN:(c + 1) * SPAN], ALU.max, ALU.mult).then_inc(weight_ready, 1)
                    if c >= 1:
                        if j == 3:
                            dve.wait_ge(weight_used, c * T)
                            att_scalars(c - 1)
                        if 4 <= j < 4 + SPAN_TILES:
                            att_tile(c - 1, j - 4)
                        if j == STD_AT + 2:
                            att_rstd(c - 1)
                        if j >= T - SPAN_TILES:
                            att_norm(c - 1, j - (T - SPAN_TILES))
            dve.wait_ge(weight_used, SPANS * T)
            att_scalars(SPANS - 1)
            for t in range(SPAN_TILES):
                att_tile(SPANS - 1, t)
            att_rstd(SPANS - 1)
            for t in range(SPAN_TILES):
                att_norm(SPANS - 1, t)

            dve.wait_ge(flag_ready, 1)
            with dve.If(dve.value_load(flag[0:1, 0:1], min_val=0, max_val=1)):
                taken = [0, 0]

                def cstep(ins):
                    taken[0] += 1
                    ins.then_inc(careful_step, 1)
                    dve.wait_ge(careful_step, taken[1] + taken[0])

                for m, opened in enumerate((careful_used[0], careful_used[1], careful_ready, careful_multiplied)):
                    piece = slice(m * T // 4, (m + 1) * T // 4)
                    ts(lift_cols[:, piece], f2_cols[:, piece], limits[:, 5:6], 1.0, ALU.add, ALU.add)\
                        .then_inc(opened, 1)
                    dve.wait_ge(opened, 1)
                dve.wait_ge(h1_ready, T)
                MAX_STEPS, WEIGH_STEPS = PAIRS * 2 * (LOAD_TILES - 1), T
                CHUNK_STEPS = SPAN_TILES - 1 + 2 + MAX_STEPS + 5 + WEIGH_STEPS + 2 * SPAN_BANKS + 1 \
                    + 4 * SPAN_TILES - 1 + 1
                for c in range(SPANS):
                    taken[:] = [0, c * CHUNK_STEPS]
                    if c >= 1:
                        dve.wait_ge(careful_done, c)
                    for t in range(SPAN_TILES):
                        one = ts(diag[:, t, :], ident[:, :], f1_cols[:, bass.ds(c * SPAN_TILES + t, 1)], None, ALU.mult)
                        if t < SPAN_TILES - 1:
                            cstep(one)
                    one.then_inc(diag_ready, 1)
                    dve.wait_ge(f1_spread, c + 1)
                    f1_row = h[:, bass.ds(c * SPAN, SPAN)]
                    for half in range(2):
                        cstep(nc.vector.tensor_copy(h[:, bass.ds(c * SPAN + half * WIDE, WIDE)], bank[4 + half][:, :]))
                    dve.wait_ge(diag_ready, c + 1)
                    nc.vector.memset(run_max, 0.0).then_inc(careful_zeroed, 1)
                    dve.wait_ge(careful_zeroed, c + 1)
                    max_base = taken[1] + taken[0]
                    with dve.Fori(0, PAIRS) as pair:
                        for s in range(2):
                            dve.wait_ge(careful_in[s], (2 * c * PAIRS + pair + 1) * 16)
                            for u in range(LOAD_TILES):
                                j = pair * 2 * LOAD_TILES + s * LOAD_TILES + u
                                one = stt(run_max, stage[:, s, u, :], lift_cols[:, bass.ds(j, 1)], run_max,
                                          ALU.mult, ALU.max)
                                if u < LOAD_TILES - 1:
                                    one.then_inc(careful_step, 1)
                                    dve.wait_ge(careful_step, max_base + pair * 2 + s + 1)
                                else:
                                    one.then_inc(careful_used[s], 1)
                                    dve.wait_ge(careful_used[s], c * PAIRS + pair + 2)
                    taken[0] += MAX_STEPS
                    dve.wait_ge(row_max_ready, c + 1)
                    cstep(ts(row_max, row_max, limits[:, 5:6], 1.0, ALU.subtract, ALU.subtract))
                    cstep(tt(row_max, row_max, f1_row, ALU.add))
                    cstep(ts(run_max, row_max, SLOPE, None, ALU.mult))
                    cstep(tt(row_max, row_max, run_max, ALU.max))
                    cstep(tt(up_row, f1_row, row_max, ALU.subtract))
                    stt(f1_row, f1_row, SLOPE, row_max, ALU.mult, ALU.subtract).then_inc(rows_ready, 1)
                    dve.wait_ge(rows_ready, c + 1)
                    weigh_base = taken[1] + taken[0]
                    with dve.Fori(0, PAIRS) as pair:
                        for s in range(2):
                            dve.wait_ge(careful_in[s], ((2 * c + 1) * PAIRS + pair + 1) * 16)
                            for u in range(LOAD_TILES):
                                k = s * LOAD_TILES + u
                                dve.wait_ge(exps_ready, c * T + pair * 2 * LOAD_TILES + k + 1)
                                tt(exp_up, exp_up, exp_low, ALU.max).then_inc(careful_step, 1)
                                dve.wait_ge(careful_step, weigh_base + pair * 2 * LOAD_TILES + k + 1)
                                dve.wait_ge(careful_multiplied, c * T + pair * 2 * LOAD_TILES + k + 1)
                                stt(careful_weight, exp_up, 1.0, stage[:, s, u, :], ALU.min, ALU.mult)\
                                    .then_inc(careful_ready, 1)
                    taken[0] += WEIGH_STEPS
                    dve.wait_ge(careful_multiplied, c * T + T + 1)
                    att_scalars(0, cstep)
                    dve.wait_ge(careful_x_in, c * 16 + 16)
                    for t in range(SPAN_TILES):
                        cstep(stt(mix, xsum[:, :], isolated[:, t:t + 1], att_acc(0, t, slice(0, D)), ALU.mult, ALU.add))
                        cstep(stt(xr[:, t, :], mix, inv_denom[:, t:t + 1], xr[:, t, :], ALU.mult, ALU.add))
                        cstep(nc.vector.bn_stats(stats[:, 0:6], xr[:, t, :]))
                        one = nc.vector.bn_aggr(mv3[:, t, :], stats[:, 0:6])
                        if t < SPAN_TILES - 1:
                            cstep(one)
                    one.then_inc(careful_var, 1)
                    dve.wait_ge(careful_var, c + 1)
                    dve.wait_ge(careful_std, c + 1)
                    cstep(nc.vector.reciprocal(rstd[:, :], std[:, :]))
                    for t in range(SPAN_TILES):
                        one = ts(h3d[:, bass.ds(c * SPAN_TILES + t, 1), :], xr[:, t:t + 1, :], mv3[:, t, 0:1],
                                 rstd[:, t:t + 1], ALU.subtract, ALU.mult)
                    one.then_inc(careful_done, 1)
                    assert taken[0] == CHUNK_STEPS, taken[0]

            step(nc.vector.memset(gparts[:, :, 2 * D:GW], 1.0))
            for m in range(QUADS):
                quad = slice(m * QUAD, (m + 1) * QUAD)
                dve.wait_ge(g_copied, m + 1)
                g_psum = bank[4 + m % 2][:, :].rearrange("p (t d) -> p t d", t=QUAD)
                step(ts(gparts[:, quad, 0:D], g_psum, S_G, None, ALU.mult))
                stt(gparts[:, quad, D:2 * D], g_psum, S_G, gparts[:, quad, 0:D], ALU.mult, ALU.subtract)\
                    .then_inc(g_low_ready, 1)

            def layer_norm(rows_in, k, ready):
                for t in range(k):
                    step(nc.vector.bn_stats(stats[:, 0:6], rows_in(t)))
                    last = nc.vector.bn_aggr(mv3[:, t, :], stats[:, 0:6])
                    if t < k - 1:
                        step(last)
                last.then_inc(ready, 1)

            def diff_slot(t):
                return tmp[:, 512 + t % 2 * D:512 + (t % 2 + 1) * D]

            def diff_tile(t):
                p = bank[t % 4]
                low = tmp[:, t % 2 * DX:(t % 2 + 1) * DX]
                dve.wait_ge(diff_low, t + 1)
                step(nc.vector.tensor_copy(deg[:, t:t + 1], low[:, D:DX]))
                step(ts(small[:, 0:1], deg[:, t:t + 1], alpha_col, ONE_MINUS_A, ALU.mult, ALU.add))
                step(ts(small[:, 1:2], small[:, 0:1], 0.0, None, ALU.is_equal))
                step(tt(small[:, 2:3], small[:, 0:1], small[:, 1:2], ALU.add))
                step(nc.vector.reciprocal(small[:, 3:4], small[:, 2:3]))
                step(ts(small[:, 4:5], small[:, 1:2], -1.0, 1.0, ALU.mult, ALU.add))
                step(stt(small[:, 5:6], small[:, 3:4], small[:, 4:5], INV_SG, ALU.mult, ALU.mult))
                s = diff_slot(t)
                tt(s, p[:, 0:D], low[:, 0:D], ALU.add).then_inc(diff_read, 1)
                dve.wait_ge(diff_read, t + 1)
                step(stt(s, s, alpha_col, g_own[:, t, :], ALU.mult, ALU.add))
                step(stt(s, s, small[:, 5:6], bias_row, ALU.mult, ALU.add))
                step(stt(s, s, 0.0, h3d[:, t, :], ALU.max, ALU.add))
                step(nc.vector.bn_stats(stats[:, 0:6], s))
                nc.vector.bn_aggr(mv3[:, t % 2, :], stats[:, 0:6]).then_inc(var1_ready, 1)
                dve.wait_ge(var1_ready, t + 1)

            def diff_norm(t):
                dve.wait_ge(std1_ready, t + 1)
                step(nc.vector.reciprocal(rstd[:, 0:1], std[:, t % 2:t % 2 + 1]))
                ts(h3d[:, t, :], diff_slot(t), mv3[:, t % 2, 0:1], rstd[:, 0:1], ALU.subtract, ALU.mult)\
                    .then_inc(h2_ready, 1)
                dve.wait_ge(h2_ready, t + 1)

            def b4_parts(m):
                dve.wait_ge(b4_done, m + 1)
                step(nc.vector.tensor_copy(parts[1][:, m, 0, :], bank[6 + m % 2][:, :]))
                tt(parts[1][:, m, 1, :], bank[6 + m % 2][:, :], parts[1][:, m, 0, :], ALU.subtract)\
                    .then_inc(parts_ready, 1)

            for t in range(T):
                diff_tile(t)
                if t >= 1:
                    diff_norm(t - 1)
                if t >= 7 and t % QUAD == 3:
                    b4_parts((t - 7) // QUAD)
            diff_norm(T - 1)
            nc.vector.reduce_max(small[:, 8:9], deg[:, :], AX.X).then_inc(deg_max, 1)
            dve.wait_ge(pool_reduced, 1)
            step(ts(small[:, 10:11], small[:, 9:10], 4.0, 4.0, ALU.mult, ALU.add))
            step(ts(GROW.bitcast(i32), small[:, 10:11].bitcast(i32), EXPONENT_BITS, None, ALU.bitwise_and))
            step(nc.vector.reciprocal(INV_GROW, GROW))
            for k in (3, 2, 1):
                step(tt(S_K[k], S_K[k + 1], INV_GROW, ALU.mult))
            step(ts(EV, INV_GROW, 2.0, None, ALU.mult))
            step(stt(SUB, INV_GROW, -1.0, INV_GROW, ALU.mult, ALU.mult))
            step(nc.vector.reciprocal(EV0, S_K[1]))
            step(nc.vector.reciprocal(SUB0, S_K[2]))
            step(ts(SUB0, SUB0, -1.0, None, ALU.mult))
            for k in (3, 2, 1):
                step(ts(th_scaled[:, (3 - k) * D:(4 - k) * D], th[:, k * D:(k + 1) * D], S_K[k + 1], 0.5,
                        ALU.mult, ALU.mult))
            step(tt(th[:, 0:D], th[:, 0:D], ident[:, :], ALU.add))
            ts(th_scaled[:, 3 * D:4 * D], th[:, 0:D], S_K[1], None, ALU.mult).then_inc(theta_ready, 1)
            b4_parts(QUADS - 1)

            for q in range(ORDERS):
                k = ORDERS - 2 - q
                dst = parts[q % 2]
                for c in range(QUADS):
                    n = q * QUADS + c
                    back = bank[2 + n % 2][:, :]
                    if k >= 0 and k <= 2:
                        step(tt(old_b, dst[:, c, 0, :], dst[:, c, 1, :], ALU.add))
                    if k < 0:
                        step(tt(old_b, parts[1][:, c, 0, :], parts[1][:, c, 1, :], ALU.add))
                    dve.wait_ge(back_done, n + 1)
                    if k == 3:
                        nc.vector.tensor_copy(new_b, back).then_inc(back_read, 1)
                    else:
                        minus = SUB if k >= 1 else SUB0 if k == 0 else 1.0
                        stt(new_b, old_b, minus, back, ALU.mult, ALU.add).then_inc(back_read, 1)
                    dve.wait_ge(back_read, n + 1)
                    if k <= 0:
                        layer_norm(lambda t: new_b[:, t * D:(t + 1) * D], QUAD, var2_ready)
                        r = (q - ORDERS + 2) * QUADS + c
                        dve.wait_ge(std2_ready, r + 1)
                        step(nc.vector.reciprocal(rstd[:, 0:QUAD], std[:, 0:QUAD]))
                        if k < 0 and c >= 2:
                            dve.wait_ge(out_stored[c % 2], 16 * (c // 2))
                        dst_rows = new_b if k == 0 else out_slot(c)
                        for t in range(QUAD):
                            one = ts(dst_rows[:, t * D:(t + 1) * D], new_b[:, t * D:(t + 1) * D], mv3[:, t, 0:1],
                                     rstd[:, t:t + 1], ALU.subtract, ALU.mult)
                            if k == 0 or t < QUAD - 1:
                                step(one)
                        if k < 0:
                            one.then_inc(out_ready, 1)
                            continue
                    step(nc.vector.tensor_copy(dst[:, c, 0, :], new_b))
                    tt(dst[:, c, 1, :], new_b, dst[:, c, 0, :], ALU.subtract).then_inc(parts_ready, 1)
                    dve.wait_ge(parts_ready, (q + 1) * QUADS + c + 1)

        @block.tensor
        def _(pe):
            mm = nc.tensor.matmul
            pe.wait_ge(weights_in[0], 16)
            pe.wait_ge(weights_in[1], 16)
            for e in range(2):
                last = mm(bank[6][:, 2 * e:2 * e + 2], w1_sb[:, e * P:(e + 1) * P], w23_sb[:, :], start=True, stop=True)
            last.then_inc(v_done, 1)
            pe.wait_ge(w2_wide_ready, 1)
            for e in range(2):
                last = mm(bank[7][:, e * P:(e + 1) * P], w1_sb[:, e * P:(e + 1) * P], w2_wide, start=True, stop=True)
            last.then_inc(v_done, 1)
            pe.wait_ge(v_ready, 1)
            pe.wait_ge(in2_in[0], 16)
            pe.wait_ge(in2_in[1], 16)
            for t in range(T):
                for e in range(2):
                    last = mm(bank[6][:, 64 + 2 * t:66 + 2 * t], in2[:, e, t * P:(t + 1) * P],
                              v_cols[:, 2 * e:2 * e + 2], start=(e == 0), stop=(e == 1))
            last.then_inc(f_cols_done, 1)
            pe.wait_ge(v_ready, 2)
            for c in range(QUADS):
                if c >= 4:
                    pe.wait_ge(f1_row_ready, c - 3)
                for e in range(2):
                    last = mm(bank[c % 4][:, :], v1_wide[:, e, :], in2[:, e, c * WIDE:(c + 1) * WIDE],
                              start=(e == 0), stop=(e == 1))
                last.then_inc(f1_row_done, 1)
            pe.wait_ge(squares_ready, 1)
            mm(bank[5][:, :], ones[:, :], squares[:, 0:WIDE], start=True, stop=True)
            mm(bank[4][:, 0:2 * D], ones[:, :], squares[:, WIDE:WIDE + 2 * D], start=True, stop=True)\
                .then_inc(norms_done, 1)
            pe.wait_ge(x_in, 16)
            for t in range(T):
                last = mm(bank[7][:, 0:D], ones[:, :], x3[:, t, 0:D], start=(t == 0), stop=(t == T - 1))
            last.then_inc(xsum_done, 1)

            pe.wait_ge(f1_row_ready, QUADS)
            pe.wait_ge(part_scale_var, 1)
            UNROLL = 4

            def weigh(c, j, k):
                first = k == 0 and j is k
                pe.wait_ge(weight_ready, j + (c * T + 1))
                for t in range(SPAN_TILES):
                    x_tile = x3[:, bass.ds(j, 1), :].rearrange("p a d -> p (a d)")
                    last = mm(att_acc(c, t), weight[:, k % 2, t * P:(t + 1) * P], x_tile,
                              start=(first and t % PER_BANK == 0), stop=False, skip_group_check=True)
                last.then_inc(weight_used, 1)

            for c in range(SPANS):
                if c >= 2:
                    pe.wait_ge(h1_ready, SPAN_TILES * (c - 1))
                for j in range(UNROLL):
                    weigh(c, j, j)
                with pe.Fori(1, T // UNROLL) as group:
                    for k in range(UNROLL):
                        weigh(c, group * UNROLL + k, k)

            pe.wait_ge(flag_ready, 1)
            with pe.If(pe.value_load(flag[0:1, 0:1], min_val=0, max_val=1)):
                for c in range(SPANS):
                    pe.wait_ge(diag_ready, c + 1)
                    for t in range(SPAN_TILES):
                        b, o = 4 + t // QUAD, t % QUAD * P
                        last = mm(bank[b][:, o:o + P], ones[:, :], diag[:, t, :], start=True, stop=True)
                    last.then_inc(f1_spread, 1)
                    for j0, count in ((0, 1), (1, T - 1)):
                        with pe.Fori(j0, j0 + count) as j:
                            pe.wait_ge(careful_ready, c * T + j + 2)
                            for t in range(SPAN_TILES):
                                last = mm(att_acc(0, t), careful_weight[:, t * P:(t + 1) * P],
                                          x3[:, bass.ds(j, 1), :].rearrange("p a d -> p (a d)"),
                                          start=(j0 == 0 and t % PER_BANK == 0), stop=False, skip_group_check=True)
                            last.then_inc(careful_multiplied, 1)
                pe.wait_ge(careful_done, SPANS)

            def turn(m, b):
                for t in range(QUAD):
                    last = nc.tensor.transpose(bank[b][:, t * D:(t + 1) * D], h3d[:, m * QUAD + t, :], ident[:, :])
                return last

            def project(m):
                pe.wait_ge(turn_copied, m + 1)
                if m >= 2:
                    pe.wait_ge(g_low_ready, m - 1)
                for t in range(QUAD):
                    o = m % 2 * WIDE + t * P
                    last = mm(bank[4 + m % 2][:, t * D:(t + 1) * D], tmp[:, o:o + P], wt_sb[:, :], start=True, stop=True)
                last.then_inc(g_done, 1)

            pe.wait_ge(h1_ready, T)
            for m in range(QUADS):
                if m >= 2:
                    pe.wait_ge(turn_copied, m - 1)
                turn(m, m % 2).then_inc(turn_done, 1)
                if m >= 1:
                    project(m - 1)
            project(QUADS - 1)

            def turn_h2(m):
                pe.wait_ge(h2_ready, (m + 1) * QUAD)
                if m >= 2:
                    pe.wait_ge(h2t_copied, m - 1)
                turn(m, 4 + m % 2).then_inc(h2t_done, 1)

            def start_b4(m):
                pe.wait_ge(h2t_copied, m + 1)
                if m >= 2:
                    pe.wait_ge(parts_ready, m - 1)
                for t in range(QUAD):
                    o = (m * QUAD + t) * P
                    last = mm(bank[6 + m % 2][:, t * D:(t + 1) * D], h2t[:, o:o + P], th[:, (ORDERS - 1) * D:],
                              start=True, stop=True)
                last.then_inc(b4_done, 1)

            for t in range(T):
                if t >= 4:
                    pe.wait_ge(diff_read, t - 3)
                for j in range(T):
                    if t == 0 and j % QUAD == 0:
                        pe.wait_ge(g_low_ready, j // QUAD + 1)
                    last = mm(bank[t % 4][:, 0:GW], adj3[:, j, t * P:(t + 1) * P], gparts[:, j, :],
                              start=(j == 0), stop=(j == T - 1))
                last.then_inc(diff_done, 1)
                if t >= 5 and t % QUAD == 1:
                    turn_h2(t // QUAD - 1)
                if t >= 6 and t % QUAD == 2:
                    start_b4(t // QUAD - 1)
            turn_h2(QUADS - 1)
            start_b4(QUADS - 1)

            def turn_back(n):
                pe.wait_ge(acc_copied, n + 1)
                if n >= 2:
                    pe.wait_ge(back_read, n - 1)
                for t in range(QUAD):
                    last = nc.tensor.transpose(bank[2 + n % 2][:, t * D:(t + 1) * D],
                                               turned_slot(n)[:, t * P:(t + 1) * P], ident[:, :])
                last.then_inc(back_done, 1)

            pe.wait_ge(diff_read, T)
            for q in range(ORDERS):
                src = parts[(q + 1) % 2]
                plain = q == ORDERS - 1
                for c in range(QUADS):
                    n = q * QUADS + c
                    if n >= 2:
                        pe.wait_ge(acc_copied, n - 1)
                    for j in range(T):
                        if c == 0 and j % QUAD == 0:
                            pe.wait_ge(parts_ready, q * QUADS + j // QUAD + 1)
                        for part in range(2):
                            last = mm(bank[n % 2][:, :], src[:, j // QUAD, part, j % QUAD * P:(j % QUAD + 1) * P],
                                      adj3[:, j, c * WIDE:(c + 1) * WIDE], start=(j == 0 and part == 0),
                                      stop=(plain and j == T - 1 and part == 1))
                        if j == 3 and c >= 1:
                            turn_back(n - 1)
                    if not plain:
                        if n == 0:
                            pe.wait_ge(theta_ready, 1)
                        last = mm(bank[n % 2][:, :], th_scaled[:, q * D:(q + 1) * D], h2t[:, c * WIDE:(c + 1) * WIDE],
                                  start=False, stop=True)
                    last.then_inc(acc_done, 1)
                turn_back(q * QUADS + QUADS - 1)


_SHAPES = dict(n=4096, tiles=32, p=128, spans=4, loads=16, pair=2, span=1024)


def kernel(x, adj, L0_gnn_inlayer2, L0_gnn_W1, L0_gnn_w2, L0_gnn_b2, L0_gnn_w3, L0_gnn_b3, L1_gnn_t, L1_gnn_alpha,
           L1_gnn_W, L1_gnn_b, L2_gnn_theta):
    import numpy as _np
    import concourse.bacc as _bacc
    from concourse import mybir as _mybir
    from concourse.bass_utils import run_bass_kernel_spmd as _run

    s = _SHAPES
    host = lambda a: _np.asarray(a)
    adj = host(adj)
    blocks = adj.T.reshape(s["loads"], s["pair"], s["p"], s["spans"], s["span"]).transpose(3, 0, 2, 1, 4)
    nodes = host(x).reshape(s["tiles"], s["p"], -1).transpose(1, 0, 2)
    in2_t = host(L0_gnn_inlayer2).T.reshape(2, s["p"], s["n"]).transpose(1, 0, 2)
    row = _np.concatenate([host(L0_gnn_b2).reshape(1), host(L0_gnn_b3).reshape(1), host(L1_gnn_alpha).reshape(1),
                           host(L1_gnn_b)])
    arrays = {
        "adj_blocks": blocks,
        "x_nodes": nodes,
        "in2_t": in2_t,
        "w1": host(L0_gnn_W1),
        "w23": _np.stack([host(L0_gnn_w2), host(L0_gnn_w3)], axis=1),
        "wt": host(L1_gnn_W).T,
        "theta": host(L2_gnn_theta).transpose(1, 0, 2),
        "row_params": _np.broadcast_to(row, (s["p"], row.shape[0])),
    }
    arrays = {k: _np.ascontiguousarray(v) for k, v in arrays.items()}
    nc = _bacc.Bacc("TRN2", target_bir_lowering=False, num_devices=1)
    args = [nc.dram_tensor(k, v.shape, _mybir.dt.from_np(v.dtype), kind="ExternalInput").ap() for k, v in arrays.items()]
    out = nc.dram_tensor("out", (s["n"], s["p"]), _mybir.dt.float32, kind="ExternalOutput").ap()
    gnn_kernel(nc, *args, out)
    return _run(nc, [arrays], core_ids=[0]).results[0]["out"]
```

```python
from contextlib import ExitStack

import numpy as np

import concourse.bass as bass
from concourse import mybir


def gnn_kernel(nc, adj_blocks, x_nodes, in2_t, w1, w23, wt, theta, row_params, out):
    fp32 = mybir.dt.float32
    fp16 = mybir.dt.float16
    fp8 = mybir.dt.float8e4
    i32 = mybir.dt.int32
    ALU = mybir.AluOpType
    ACT = mybir.ActivationFunctionType
    AX = mybir.AxisListType
    RMAX = bass.bass_isa.ReduceOp.max

    N = 4096
    D = 128
    P = 128
    T = N // P
    ORDERS = theta.shape[1]
    EPS = 1e-5
    SLOPE = 0.01
    TAU = 0.5
    COEFF = [2.0 / ORDERS * float(np.exp(-TAU * np.cos(np.pi * (k + 0.5) / ORDERS))) for k in range(ORDERS)]
    EXPONENT_BITS = 0x7F800000
    PART_TOP = 2.0 ** 15
    TINY = 1e-30

    PAIRS = 8
    LOGIT_LIMIT = 32.0
    LOW_LIMIT = 4000.0

    SPAN = 1024
    SPANS = N // SPAN
    SPAN_TILES = SPAN // P
    LOAD_TILES = 2
    LOADS = SPANS * T // LOAD_TILES
    LOADS_PER_SPAN = T // LOAD_TILES
    SLOTS = 4
    ADJ_SEMS = 8
    DX = D + 1
    PER_BANK = 3
    SPAN_BANKS = -(-SPAN_TILES // PER_BANK)
    QUAD = 4
    QUADS = T // QUAD
    WIDE = QUAD * D
    GW = 2 * D + 1

    with ExitStack() as ctx:
        def sb(name, shape, dt=fp32):
            return ctx.enter_context(nc.sbuf_tensor(name, shape, dt))

        def sem(name):
            return ctx.enter_context(nc.semaphore(name))

        adj8 = sb("adj8", [P, T * N], fp8)
        adj3 = adj8[:, :].rearrange("p (t n) -> p t n", t=T)
        in2 = adj8[:, (T - 8) * N:].bitcast(fp32).rearrange("p (e n) -> p e n", e=2)
        xh = sb("xh", [P, T * DX])
        x3 = xh[:, :].rearrange("p (t d) -> p t d", t=T)
        h2t = xh[:, 0:N]
        h = sb("h", [P, N])
        h3d = h[:, :].rearrange("p (t d) -> p t d", t=T)
        work = sb("work", [P, 8208])
        expo = work[:, 0:SLOTS * SPAN].rearrange("p (s n) -> p s n", s=SLOTS)
        weight = work[:, SLOTS * SPAN:2 * SLOTS * SPAN].rearrange("p (s n) -> p s n", s=SLOTS)
        gparts = work[:, 0:T * GW // 2].bitcast(fp16).rearrange("p (t w) -> p t w", t=T)
        g_own = work[:, 4112:4112 + N].rearrange("p (t d) -> p t d", t=T)
        parts = [work[:, base:base + N].bitcast(fp16).rearrange("p (m q w) -> p m q w", m=QUADS, q=2)
                 for base in (0, 4112)]
        tmp = sb("tmp", [P, QUAD * DX + 2 * WIDE])
        xr = tmp[:, 0:SPAN_TILES * D].rearrange("p (t d) -> p t d", t=SPAN_TILES)
        mix = tmp[:, 1024:1024 + D]
        v_cols = tmp[:, 0:4]
        v1_wide = tmp[:, 512:512 + 2 * P].rearrange("p (e n) -> p e n", e=2)
        w2_wide = tmp[:, 1024:1024 + P]
        squares = tmp[:, 0:(ORDERS + 1) * D]
        w1_sb = sb("w1_sb", [P, 2 * P])
        w23_sb = sb("w23_sb", [P, 2])
        wt_sb = sb("wt_sb", [P, D])
        th = sb("th", [P, ORDERS * D])
        th_scaled = sb("th_scaled", [P, (ORDERS - 1) * D])
        rows = sb("rows", [P, 3 + D])
        b2_col, b3_col, alpha_col, bias_row = rows[:, 0:1], rows[:, 1:2], rows[:, 2:3], rows[:, 3:3 + D]
        ident = sb("ident", [P, P])
        ones = sb("ones", [P, P])
        xsum = sb("xsum", [P, D])
        f1_cols = sb("f1_cols", [P, T])
        f2_cols = sb("f2_cols", [P, T])
        q_cols = sb("q_cols", [P, T])
        low_cols = sb("low_cols", [P, T])
        eps_col = sb("eps_col", [P, 1])
        isolated = sb("isolated", [P, SPAN_TILES])
        denom = sb("denom", [P, SPAN_TILES])
        inv_denom = sb("inv_denom", [P, SPAN_TILES])
        stats = sb("stats", [P, 6 * QUAD])
        inv_deg = sb("inv_deg", [P, QUAD])
        no_deg = sb("no_deg", [P, QUAD])
        mv = sb("mv", [P, 2 * SPAN_TILES])
        mv3 = mv[:, :].rearrange("p (t k) -> p t k", k=2)
        std = sb("std", [P, SPAN_TILES])
        rstd = sb("rstd", [P, SPAN_TILES])
        deg = sb("deg", [P, T])
        limits = sb("limits", [P, 8])
        flag = sb("flag", [P, 1], i32)
        lift_cols = sb("lift_cols", [P, T])
        stage = work[:, 0:2 * LOAD_TILES * SPAN].rearrange("p (s t n) -> p s t n", s=2, t=LOAD_TILES)
        diag = work[:, 4096:4096 + SPAN].rearrange("p (t n) -> p t n", t=SPAN_TILES)
        run_max = work[:, 4096:4096 + SPAN]
        row_max = work[:, 5120:5120 + SPAN]
        exp_up, exp_low = run_max, row_max
        careful_weight = work[:, 6144:6144 + SPAN]
        up_row = work[:, 7168:7168 + SPAN]
        small = sb("small", [P, 16])
        scales = sb("scales", [P, 16])
        S_G, INV_SG, ONE_MINUS_A, S4, GROW, INV_GROW = [scales[:, n:n + 1] for n in range(6)]
        OWN = scales[:, 13:14]
        EV, SUB, EV0, SUB0 = [scales[:, n:n + 1] for n in range(6, 10)]
        S_K = {4: S4, 3: scales[:, 10:11], 2: scales[:, 11:12], 1: scales[:, 12:13]}

        bank = [ctx.enter_context(nc.psum_tensor(f"bank{n}", [P, WIDE], fp32)) for n in range(8)]

        weights_in = [sem(f"weights_in{n}") for n in range(6)]
        in2_in = [sem("in2_in0"), sem("in2_in1")]
        x_in = sem("x_in")
        adj_in = [sem(f"adj_in{n}") for n in range(ADJ_SEMS)]
        xr_in = sem("xr_in")
        out_stored = [sem("out_stored0"), sem("out_stored1")]
        const_ready = sem("const_ready")
        pool_reduced = sem("pool_reduced")
        act_step = sem("act_step")
        dve_step = sem("dve_step")
        w2_wide_ready = sem("w2_wide_ready")
        v_done = sem("v_done")
        v_ready = sem("v_ready")
        f_cols_done = sem("f_cols_done")
        f_cols_ready = sem("f_cols_ready")
        f1_row_done = sem("f1_row_done")
        f1_row_ready = sem("f1_row_ready")
        squares_ready = sem("squares_ready")
        norms_done = sem("norms_done")
        part_scale_var = sem("part_scale_var")
        part_scale_root = sem("part_scale_root")
        part_scales_ready = sem("part_scales_ready")
        xsum_done = sem("xsum_done")
        q_ready = sem("q_ready")
        limits_ready = sem("limits_ready")
        limits_reduced = sem("limits_reduced")
        flag_ready = sem("flag_ready")
        careful_x_in = sem("careful_x_in")
        careful_in = [sem("careful_in0"), sem("careful_in1")]
        careful_used = [sem("careful_used0"), sem("careful_used1")]
        careful_step = sem("careful_step")
        diag_ready = sem("diag_ready")
        f1_spread = sem("f1_spread")
        row_max_ready = sem("row_max_ready")
        rows_ready = sem("rows_ready")
        exps_ready = sem("exps_ready")
        careful_ready = sem("careful_ready")
        careful_multiplied = sem("careful_multiplied")
        careful_var = sem("careful_var")
        careful_std = sem("careful_std")
        careful_done = sem("careful_done")
        careful_zeroed = sem("careful_zeroed")
        expo_ready = sem("expo_ready")
        weight_ready = sem("weight_ready")
        weight_used = sem("weight_used")
        var_ready = sem("var_ready")
        std_ready = sem("std_ready")
        h1_ready = sem("h1_ready")
        turn_done = sem("turn_done")
        turn_copied = sem("turn_copied")
        g_done = sem("g_done")
        g_copied = sem("g_copied")
        g_low_ready = sem("g_low_ready")
        diff_done = sem("diff_done")
        diff_low = sem("diff_low")
        diff_read = sem("diff_read")
        var1_ready = sem("var1_ready")
        std1_ready = sem("std1_ready")
        h2_ready = sem("h2_ready")
        h2t_done = sem("h2t_done")
        h2t_copied = sem("h2t_copied")
        b4_done = sem("b4_done")
        parts_ready = sem("parts_ready")
        deg_max = sem("deg_max")
        theta_ready = sem("theta_ready")
        acc_done = sem("acc_done")
        acc_copied = sem("acc_copied")
        back_done = sem("back_done")
        back_read = sem("back_read")
        var2_ready = sem("var2_ready")
        std2_ready = sem("std2_ready")
        out_ready = sem("out_ready")

        block = ctx.enter_context(nc.Block())

        def adj_target(load):
            c, j = load // LOADS_PER_SPAN, load % LOADS_PER_SPAN * LOAD_TILES
            return adj3[:, j:j + LOAD_TILES, c * SPAN:(c + 1) * SPAN]

        def wait_adj(eng, load):
            eng.wait_ge(adj_in[load % ADJ_SEMS], 16 * (load // ADJ_SEMS + 1))

        def att_acc(c, t, cols=slice(0, DX)):
            b = SPAN_BANKS * (c % 2) + t // PER_BANK
            base = t % PER_BANK * DX
            return bank[b][:, base + cols.start:base + cols.stop]

        LIMITS_AT = 24
        STD_AT = 20

        def low_slot(t):
            return tmp[:, t % QUAD * DX:(t % QUAD + 1) * DX]

        def turned_slot(c):
            return h[:, c % 2 * WIDE:(c % 2 + 1) * WIDE]

        def out_slot(c):
            return h[:, (2 + c % 2) * WIDE:(3 + c % 2) * WIDE]

        old_b = h[:, 4 * WIDE:5 * WIDE]
        new_b = h[:, 5 * WIDE:6 * WIDE]

        @block.sync
        def _(sp):
            for e in range(2):
                sp.dma_start(in2[:, e, :], in2_t[:, e, :]).then_inc(in2_in[e], 16)
            sp.dma_start(x3[:, :, 0:D], x_nodes).then_inc(x_in, 16)

            def load_residual(c):
                if c >= 1:
                    sp.wait_ge(h1_ready, SPAN_TILES * c)
                else:
                    sp.wait_ge(norms_done, 1)
                sp.dma_start(xr, x_nodes[:, c * SPAN_TILES:(c + 1) * SPAN_TILES, :]).then_inc(xr_in, 16)

            for c in range(SPANS):
                load_residual(c)

            sp.wait_ge(flag_ready, 1)
            with sp.If(sp.value_load(flag[0:1, 0:1], min_val=0, max_val=1)):
                sp.wait_ge(h1_ready, T)
                for c in range(SPANS):
                    if c >= 1:
                        sp.wait_ge(careful_done, c)
                    sp.dma_start(xr, x_nodes[:, bass.ds(c * SPAN_TILES, SPAN_TILES), :]).then_inc(careful_x_in, 16)
                    for sweep in range(2):
                        if sweep == 1:
                            for s in range(2):
                                sp.wait_ge(careful_used[s], (c + 1) * PAIRS + 1)
                        with sp.Fori(0, PAIRS) as pair:
                            for s in range(2):
                                source = sp.snap(pair * 2 + s)
                                if sweep == 0:
                                    sp.wait_ge(careful_used[s], c * PAIRS + pair + 1)
                                else:
                                    sp.wait_ge(careful_ready, c * T + pair * 2 * LOAD_TILES + 1)
                                sp.dma_start(stage[:, s, :, :], adj_blocks[c, source, :, :, :])\
                                    .then_inc(careful_in[s], 16)
            out_tiles = out.rearrange("(t p) d -> p t d", p=P)
            for c in range(QUADS):
                sp.wait_ge(out_ready, c + 1)
                sp.dma_start(out_tiles[:, c * QUAD:(c + 1) * QUAD, :],
                             out_slot(c).rearrange("p (t d) -> p t d", t=QUAD)).then_inc(out_stored[c % 2], 16)
            for s in range(2):
                sp.wait_ge(out_stored[s], 16 * QUADS // 2)

        @block.gpsimd
        def _(pool):
            nc.gpsimd.memset(ones[:, :], 1.0).then_inc(const_ready, 1)
            nc.gpsimd.memset(eps_col[:, :], EPS).then_inc(const_ready, 1)
            nc.gpsimd.memset(ident[:, :], 0.0).then_inc(const_ready, 1)
            pool.wait_ge(const_ready, 3)
            nc.gpsimd.affine_select(out=ident[:, :], in_=ident[:, :], compare_op=ALU.not_equal, fill=1.0,
                                    base=0, pattern=[[-1, P]], channel_multiplier=1).then_inc(const_ready, 1)
            nc.gpsimd.memset(x3[:, :, D:DX], 1.0).then_inc(const_ready, 1)

            for load in range(LOADS):
                if load == LOADS_PER_SPAN - 4:
                    pool.wait_ge(f1_row_done, QUADS)
                if load >= ADJ_SEMS:
                    wait_adj(pool, load - ADJ_SEMS)
                pool.dma_start(adj_target(load), adj_blocks[load // LOADS_PER_SPAN, load % LOADS_PER_SPAN, :, :, :])\
                    .then_inc(adj_in[load % ADJ_SEMS], 16)
                if load == LIMITS_AT:
                    pool.wait_ge(limits_ready, 1)
                    nc.gpsimd.partition_all_reduce(limits[:, 4:6], limits[:, 2:4], P, RMAX)\
                        .then_inc(limits_reduced, 1)
            pool.wait_ge(flag_ready, 1)
            with pool.If(pool.value_load(flag[0:1, 0:1], min_val=0, max_val=1)):
                for c in range(SPANS):
                    pool.wait_ge(careful_used[1], (c + 1) * PAIRS + 1)
                    nc.gpsimd.partition_all_reduce(row_max, run_max, P, RMAX).then_inc(row_max_ready, 1)
            pool.wait_ge(deg_max, 1)
            nc.gpsimd.partition_all_reduce(small[:, 9:10], small[:, 8:9], P, RMAX).then_inc(pool_reduced, 1)

        @block.scalar
        def _(act):
            for n, (dst, src) in enumerate(((w1_sb, w1), (w23_sb, w23), (rows, row_params), (wt_sb, wt))):
                act.dma_start(dst[:, :], src).then_inc(weights_in[n], 16)
            act.dma_start(th[:, :], theta.rearrange("p k d -> p (k d)")).then_inc(weights_in[4], 16)

            act.wait_ge(v_done, 1)
            nc.scalar.copy(v_cols, bank[6][:, 0:4]).then_inc(v_ready, 1)
            act.wait_ge(v_done, 2)
            nc.scalar.copy(v1_wide, bank[7][:, 0:2 * P].rearrange("p (e n) -> p e n", e=2)).then_inc(v_ready, 1)
            act.wait_ge(weights_in[2], 16)
            for c in range(QUADS):
                act.wait_ge(f1_row_done, c + 1)
                nc.scalar.activation(h[:, c * WIDE:(c + 1) * WIDE], bank[c % 4][:, :], ACT.Identity,
                                     bias=b2_col).then_inc(f1_row_ready, 1)
            act.wait_ge(part_scale_var, 1)
            nc.scalar.activation(small[:, 4:6], small[:, 2:4], ACT.Sqrt).then_inc(part_scale_root, 1)
            act.wait_ge(f_cols_ready, 1)
            act.wait_ge(f_cols_ready, 2)
            nc.scalar.activation(q_cols[:, :], f2_cols[:, :], ACT.Exp, scale=SLOPE).then_inc(q_ready, 1)

            act.wait_ge(f1_row_ready, QUADS)
            for c in range(SPANS):
                for j in range(T):
                    n = c * T + j
                    if n >= SLOTS:
                        act.wait_ge(weight_ready, n - SLOTS + 1)
                    nc.scalar.activation(expo[:, n % SLOTS, :], h[:, c * SPAN:(c + 1) * SPAN], ACT.Exp,
                                         bias=f2_cols[:, j:j + 1], scale=1.0 - SLOPE).then_inc(expo_ready, 1)
                    if c >= 1 and j == STD_AT:
                        act.wait_ge(var_ready, c)
                        nc.scalar.activation(std[:, :], mv3[:, :, 1], ACT.Sqrt, bias=eps_col[:, :])\
                            .then_inc(std_ready, 1)
            act.wait_ge(var_ready, SPANS)
            nc.scalar.activation(std[:, :], mv3[:, :, 1], ACT.Sqrt, bias=eps_col[:, :]).then_inc(std_ready, 1)

            act.wait_ge(flag_ready, 1)
            with act.If(act.value_load(flag[0:1, 0:1], min_val=0, max_val=1)):
                for c in range(SPANS):
                    act.wait_ge(rows_ready, c + 1)
                    with act.Fori(0, T) as j:
                        act.wait_ge(careful_ready, c * T + j + 1)
                        nc.scalar.activation(exp_up, up_row, ACT.Exp, bias=f2_cols[:, bass.ds(j, 1)])
                        nc.scalar.activation(exp_low, h[:, bass.ds(c * SPAN, SPAN)], ACT.Exp,
                                             bias=low_cols[:, bass.ds(j, 1)]).then_inc(exps_ready, 1)
                    act.wait_ge(careful_var, c + 1)
                    nc.scalar.activation(std[:, :], mv3[:, :, 1], ACT.Sqrt, bias=eps_col[:, :])\
                        .then_inc(careful_std, 1)

            for m in range(QUADS):
                act.wait_ge(turn_done, m + 1)
                if m >= 2:
                    act.wait_ge(g_done, m - 1)
                nc.scalar.copy(tmp[:, m % 2 * WIDE:(m % 2 + 1) * WIDE], bank[m % 2][:, :])\
                    .then_inc(turn_copied, 1)
                act.wait_ge(g_done, m + 1)
                nc.scalar.mul(g_own[:, m * QUAD:(m + 1) * QUAD, :], bank[4 + m % 2][:, :]
                              .rearrange("p (t d) -> p t d", t=QUAD), OWN).then_inc(g_copied, 1)

            for t in range(T + 4):
                if t < T:
                    act.wait_ge(diff_done, t + 1)
                    if t >= 4:
                        act.wait_ge(diff_read, t - 3)
                    nc.scalar.copy(low_slot(t), bank[t % 4][:, D:GW]).then_inc(diff_low, 1)
                if t >= QUAD and t % QUAD == 0:
                    act.wait_ge(var1_ready, t // QUAD)
                    nc.scalar.activation(std[:, 0:QUAD], mv3[:, 0:QUAD, 1], ACT.Sqrt, bias=eps_col[:, :])\
                        .then_inc(std1_ready, 1)
                if t >= 6 and t % QUAD == 2:
                    m = t // QUAD - 1
                    act.wait_ge(h2t_done, m + 1)
                    nc.scalar.copy(h2t[:, m * WIDE:(m + 1) * WIDE], bank[4 + m % 2][:, :]).then_inc(h2t_copied, 1)

            act.wait_ge(theta_ready, 1)
            for q in range(ORDERS):
                k = ORDERS - 2 - q
                for c in range(QUADS):
                    n = q * QUADS + c
                    act.wait_ge(acc_done, n + 1)
                    if n >= 2:
                        act.wait_ge(back_done, n - 1)
                    scale = EV if k >= 1 else EV0 if k == 0 else 1.0
                    nc.scalar.mul(turned_slot(n), bank[n % 2][:, :], scale).then_inc(acc_copied, 1)
                    if k <= 0:
                        r = (q - ORDERS + 2) * QUADS + c
                        act.wait_ge(var2_ready, r + 1)
                        nc.scalar.activation(std[:, 0:QUAD], mv3[:, 0:QUAD, 1], ACT.Sqrt, bias=eps_col[:, :])\
                            .then_inc(std2_ready, 1)

        @block.vector
        def _(dve):
            steps = [0]

            def step(ins):
                steps[0] += 1
                ins.then_inc(dve_step, 1)
                dve.wait_ge(dve_step, steps[0])

            tt, ts, stt = nc.vector.tensor_tensor, nc.vector.tensor_scalar, nc.vector.scalar_tensor_tensor
            dve.wait_ge(const_ready, 5)
            dve.wait_ge(weights_in[1], 16)
            ts(w2_wide, ones[:, :], w23_sb[:, 0:1], None, ALU.mult).then_inc(w2_wide_ready, 1)
            dve.wait_ge(weights_in[2], 16)
            dve.wait_ge(f_cols_done, 1)
            f_psum = bank[6][:, 64:64 + 2 * T].rearrange("p (t k) -> p t k", k=2)
            ts(f1_cols[:, :], f_psum[:, :, 0], b2_col, None, ALU.add).then_inc(f_cols_ready, 1)
            ts(f2_cols[:, :], f_psum[:, :, 1], b3_col, None, ALU.add).then_inc(f_cols_ready, 1)

            dve.wait_ge(f_cols_ready, 2)
            step(nc.vector.reduce_max(limits[:, 0:1], f1_cols[:, :], AX.X))
            step(nc.vector.reduce_max(limits[:, 1:2], f2_cols[:, :], AX.X))
            step(ts(low_cols[:, :], f2_cols[:, :], -1.0, None, ALU.mult))
            step(nc.vector.reduce_max(limits[:, 3:4], low_cols[:, :], AX.X))
            step(tt(limits[:, 0:1], limits[:, 0:1], limits[:, 1:2], ALU.max))
            stt(limits[:, 2:3], limits[:, 3:4], LOGIT_LIMIT / LOW_LIMIT, limits[:, 0:1], ALU.mult, ALU.max)\
                .then_inc(limits_ready, 1)
            dve.wait_ge(limits_ready, 1)
            step(ts(low_cols[:, :], f2_cols[:, :], SLOPE, None, ALU.mult))

            dve.wait_ge(weights_in[3], 16)
            dve.wait_ge(weights_in[4], 16)
            dve.wait_ge(f1_row_done, QUADS)
            dve.wait_ge(v_ready, 2)
            step(tt(squares[:, 0:D], wt_sb[:, :], wt_sb[:, :], ALU.mult))
            for k in range(ORDERS):
                step(ts(th[:, k * D:(k + 1) * D], th[:, k * D:(k + 1) * D], COEFF[k], None, ALU.mult))
            tt(squares[:, D:], th[:, :], th[:, :], ALU.mult).then_inc(squares_ready, 1)
            dve.wait_ge(norms_done, 1)
            step(nc.vector.reduce_max(small[:, 0:1], bank[5][:, 0:D], AX.X))
            step(nc.vector.reduce_max(small[:, 6:7], bank[5][:, D:WIDE], AX.X))
            step(nc.vector.reduce_max(small[:, 7:8], bank[4][:, 0:2 * D], AX.X))
            step(tt(small[:, 1:2], small[:, 6:7], small[:, 7:8], ALU.max))
            step(ts(small[:, 0:2], small[:, 0:2], D / PART_TOP ** 2, TINY, ALU.mult, ALU.max))
            nc.vector.reciprocal(small[:, 2:4], small[:, 0:2]).then_inc(part_scale_var, 1)
            dve.wait_ge(part_scale_root, 1)
            step(ts(small[:, 10:12].bitcast(i32), small[:, 4:6].bitcast(i32), EXPONENT_BITS, None, ALU.bitwise_and))
            step(nc.vector.tensor_copy(S_G, small[:, 10:11]))
            step(nc.vector.tensor_copy(S4, small[:, 11:12]))
            step(nc.vector.reciprocal(INV_SG, S_G))
            step(ts(ONE_MINUS_A, alpha_col, -1.0, 1.0, ALU.mult, ALU.add))
            step(tt(OWN, ONE_MINUS_A, S_G, ALU.mult))
            dve.wait_ge(xsum_done, 1)
            step(nc.vector.tensor_copy(xsum[:, :], bank[7][:, 0:D]))
            step(ts(th[:, (ORDERS - 1) * D:], th[:, (ORDERS - 1) * D:], S4, None, ALU.mult))

            def att_scalars(c, step=step):
                for b in range(SPAN_BANKS):
                    k = min(PER_BANK, SPAN_TILES - b * PER_BANK)
                    sums = bank[SPAN_BANKS * (c % 2) + b][:, 0:k * DX].rearrange("p (t w) -> p t w", w=DX)[:, :, D]
                    cols = slice(b * PER_BANK, b * PER_BANK + k)
                    step(ts(isolated[:, cols], sums, 0.0, None, ALU.is_equal))
                    step(stt(denom[:, cols], isolated[:, cols], float(N), sums, ALU.mult, ALU.add))
                step(nc.vector.reciprocal(inv_denom[:, :], denom[:, :]))

            def att_tile(c, t):
                if t == 0:
                    dve.wait_ge(xr_in, 16 * (c + 1))
                step(stt(mix, xsum[:, :], isolated[:, t:t + 1], att_acc(c, t, slice(0, D)), ALU.mult, ALU.add))
                step(stt(xr[:, t, :], mix, inv_denom[:, t:t + 1], xr[:, t, :], ALU.mult, ALU.add))
                step(nc.vector.bn_stats(stats[:, 0:6], xr[:, t, :]))
                last = nc.vector.bn_aggr(mv3[:, t, :], stats[:, 0:6])
                if t == SPAN_TILES - 1:
                    last.then_inc(var_ready, 1)
                    dve.wait_ge(var_ready, c + 1)
                else:
                    step(last)

            def att_rstd(c):
                dve.wait_ge(std_ready, c + 1)
                step(nc.vector.reciprocal(rstd[:, :], std[:, :]))

            def att_norm(c, t):
                ts(h3d[:, c * SPAN_TILES + t, :], xr[:, t, :], mv3[:, t, 0:1], rstd[:, t:t + 1],
                   ALU.subtract, ALU.mult).then_inc(h1_ready, 1)

            dve.wait_ge(q_ready, 1)
            for c in range(SPANS):
                for j in range(T):
                    n = c * T + j
                    if j % LOAD_TILES == 0:
                        wait_adj(dve, n // LOAD_TILES)
                    dve.wait_ge(expo_ready, n + 1)
                    if n >= SLOTS:
                        dve.wait_ge(weight_used, n - SLOTS + 1)
                    stt(weight[:, n % SLOTS, :], expo[:, n % SLOTS, :], q_cols[:, j:j + 1],
                        adj3[:, j, c * SPAN:(c + 1) * SPAN], ALU.max, ALU.mult).then_inc(weight_ready, 1)
                    if c >= 1:
                        if j == 3:
                            dve.wait_ge(weight_used, c * T)
                            att_scalars(c - 1)
                        if 4 <= j < 4 + SPAN_TILES:
                            att_tile(c - 1, j - 4)
                        if j == STD_AT + 2:
                            att_rstd(c - 1)
                        if j >= T - SPAN_TILES:
                            att_norm(c - 1, j - (T - SPAN_TILES))
            dve.wait_ge(limits_reduced, 1)
            ts(flag[:, :], limits[:, 4:5], LOGIT_LIMIT, None, ALU.is_gt).then_inc(flag_ready, 1)
            dve.wait_ge(weight_used, SPANS * T)
            att_scalars(SPANS - 1)
            for t in range(SPAN_TILES):
                att_tile(SPANS - 1, t)
            att_rstd(SPANS - 1)
            for t in range(SPAN_TILES):
                att_norm(SPANS - 1, t)

            dve.wait_ge(flag_ready, 1)
            with dve.If(dve.value_load(flag[0:1, 0:1], min_val=0, max_val=1)):
                taken = [0, 0]

                def cstep(ins):
                    taken[0] += 1
                    ins.then_inc(careful_step, 1)
                    dve.wait_ge(careful_step, taken[1] + taken[0])

                for m, opened in enumerate((careful_used[0], careful_used[1], careful_ready, careful_multiplied)):
                    piece = slice(m * T // 4, (m + 1) * T // 4)
                    ts(lift_cols[:, piece], f2_cols[:, piece], limits[:, 5:6], 1.0, ALU.add, ALU.add)\
                        .then_inc(opened, 1)
                    dve.wait_ge(opened, 1)
                dve.wait_ge(h1_ready, T)
                MAX_STEPS, WEIGH_STEPS = PAIRS * 2 * (LOAD_TILES - 1), T
                CHUNK_STEPS = SPAN_TILES - 1 + 2 + MAX_STEPS + 5 + WEIGH_STEPS + 2 * SPAN_BANKS + 1 \
                    + 4 * SPAN_TILES - 1 + 1
                for c in range(SPANS):
                    taken[:] = [0, c * CHUNK_STEPS]
                    if c >= 1:
                        dve.wait_ge(careful_done, c)
                    for t in range(SPAN_TILES):
                        one = ts(diag[:, t, :], ident[:, :], f1_cols[:, bass.ds(c * SPAN_TILES + t, 1)], None, ALU.mult)
                        if t < SPAN_TILES - 1:
                            cstep(one)
                    one.then_inc(diag_ready, 1)
                    dve.wait_ge(f1_spread, c + 1)
                    f1_row = h[:, bass.ds(c * SPAN, SPAN)]
                    for half in range(2):
                        cstep(nc.vector.tensor_copy(h[:, bass.ds(c * SPAN + half * WIDE, WIDE)], bank[4 + half][:, :]))
                    dve.wait_ge(diag_ready, c + 1)
                    nc.vector.memset(run_max, 0.0).then_inc(careful_zeroed, 1)
                    dve.wait_ge(careful_zeroed, c + 1)
                    max_base = taken[1] + taken[0]
                    with dve.Fori(0, PAIRS) as pair:
                        for s in range(2):
                            dve.wait_ge(careful_in[s], (2 * c * PAIRS + pair + 1) * 16)
                            for u in range(LOAD_TILES):
                                j = pair * 2 * LOAD_TILES + s * LOAD_TILES + u
                                one = stt(run_max, stage[:, s, u, :], lift_cols[:, bass.ds(j, 1)], run_max,
                                          ALU.mult, ALU.max)
                                if u < LOAD_TILES - 1:
                                    one.then_inc(careful_step, 1)
                                    dve.wait_ge(careful_step, max_base + pair * 2 + s + 1)
                                else:
                                    one.then_inc(careful_used[s], 1)
                                    dve.wait_ge(careful_used[s], c * PAIRS + pair + 2)
                    taken[0] += MAX_STEPS
                    dve.wait_ge(row_max_ready, c + 1)
                    cstep(ts(row_max, row_max, limits[:, 5:6], 1.0, ALU.subtract, ALU.subtract))
                    cstep(tt(row_max, row_max, f1_row, ALU.add))
                    cstep(ts(run_max, row_max, SLOPE, None, ALU.mult))
                    cstep(tt(row_max, row_max, run_max, ALU.max))
                    cstep(tt(up_row, f1_row, row_max, ALU.subtract))
                    stt(f1_row, f1_row, SLOPE, row_max, ALU.mult, ALU.subtract).then_inc(rows_ready, 1)
                    dve.wait_ge(rows_ready, c + 1)
                    weigh_base = taken[1] + taken[0]
                    with dve.Fori(0, PAIRS) as pair:
                        for s in range(2):
                            dve.wait_ge(careful_in[s], ((2 * c + 1) * PAIRS + pair + 1) * 16)
                            for u in range(LOAD_TILES):
                                k = s * LOAD_TILES + u
                                dve.wait_ge(exps_ready, c * T + pair * 2 * LOAD_TILES + k + 1)
                                tt(exp_up, exp_up, exp_low, ALU.max).then_inc(careful_step, 1)
                                dve.wait_ge(careful_step, weigh_base + pair * 2 * LOAD_TILES + k + 1)
                                dve.wait_ge(careful_multiplied, c * T + pair * 2 * LOAD_TILES + k + 1)
                                stt(careful_weight, exp_up, 1.0, stage[:, s, u, :], ALU.min, ALU.mult)\
                                    .then_inc(careful_ready, 1)
                    taken[0] += WEIGH_STEPS
                    dve.wait_ge(careful_multiplied, c * T + T + 1)
                    att_scalars(0, cstep)
                    dve.wait_ge(careful_x_in, c * 16 + 16)
                    for t in range(SPAN_TILES):
                        cstep(stt(mix, xsum[:, :], isolated[:, t:t + 1], att_acc(0, t, slice(0, D)), ALU.mult, ALU.add))
                        cstep(stt(xr[:, t, :], mix, inv_denom[:, t:t + 1], xr[:, t, :], ALU.mult, ALU.add))
                        cstep(nc.vector.bn_stats(stats[:, 0:6], xr[:, t, :]))
                        one = nc.vector.bn_aggr(mv3[:, t, :], stats[:, 0:6])
                        if t < SPAN_TILES - 1:
                            cstep(one)
                    one.then_inc(careful_var, 1)
                    dve.wait_ge(careful_var, c + 1)
                    dve.wait_ge(careful_std, c + 1)
                    cstep(nc.vector.reciprocal(rstd[:, :], std[:, :]))
                    for t in range(SPAN_TILES):
                        one = ts(h3d[:, bass.ds(c * SPAN_TILES + t, 1), :], xr[:, t:t + 1, :], mv3[:, t, 0:1],
                                 rstd[:, t:t + 1], ALU.subtract, ALU.mult)
                    one.then_inc(careful_done, 1)
                    assert taken[0] == CHUNK_STEPS, taken[0]

            step(nc.vector.memset(gparts[:, :, 2 * D:GW], 1.0))
            for m in range(QUADS):
                quad = slice(m * QUAD, (m + 1) * QUAD)
                dve.wait_ge(g_copied, m + 1)
                g_psum = bank[4 + m % 2][:, :].rearrange("p (t d) -> p t d", t=QUAD)
                step(ts(gparts[:, quad, 0:D], g_psum, S_G, None, ALU.mult))
                stt(gparts[:, quad, D:2 * D], g_psum, S_G, gparts[:, quad, 0:D], ALU.mult, ALU.subtract)\
                    .then_inc(g_low_ready, 1)

            def layer_norm(rows_in, k, ready):
                for t in range(k):
                    step(nc.vector.bn_stats(stats[:, 0:6], rows_in(t)))
                    last = nc.vector.bn_aggr(mv3[:, t, :], stats[:, 0:6])
                    if t < k - 1:
                        step(last)
                last.then_inc(ready, 1)

            def diff_quad(m):
                base = QUAD * DX + m % 2 * WIDE
                return tmp[:, base:base + WIDE]

            def diff_add(t):
                low = low_slot(t)
                dve.wait_ge(diff_low, t + 1)
                nc.vector.tensor_copy(deg[:, t:t + 1], low[:, D:DX])
                o = t % QUAD * D
                tt(diff_quad(t // QUAD)[:, o:o + D], bank[t % 4][:, 0:D], low[:, 0:D], ALU.add).then_inc(diff_read, 1)

            def diff_finish(m):
                s, tiles = diff_quad(m), range(m * QUAD, (m + 1) * QUAD)
                dve.wait_ge(diff_read, (m + 1) * QUAD)
                step(ts(inv_deg[:, :], deg[:, m * QUAD:(m + 1) * QUAD], alpha_col, ONE_MINUS_A, ALU.mult, ALU.add))
                step(ts(no_deg[:, :], inv_deg[:, :], 0.0, None, ALU.is_equal))
                step(tt(inv_deg[:, :], inv_deg[:, :], no_deg[:, :], ALU.add))
                step(nc.vector.reciprocal(inv_deg[:, :], inv_deg[:, :]))
                step(ts(no_deg[:, :], no_deg[:, :], -1.0, 1.0, ALU.mult, ALU.add))
                step(stt(inv_deg[:, :], inv_deg[:, :], INV_SG, no_deg[:, :], ALU.mult, ALU.mult))
                own = g_own[:, m * QUAD:(m + 1) * QUAD, :].rearrange("p t d -> p (t d)")
                step(stt(s, s, alpha_col, own, ALU.mult, ALU.add))
                for u in range(QUAD):
                    last = stt(s[:, u * D:(u + 1) * D], s[:, u * D:(u + 1) * D], inv_deg[:, u:u + 1], bias_row,
                               ALU.mult, ALU.add)
                step(last)
                step(stt(s, s, 0.0, h[:, m * WIDE:(m + 1) * WIDE], ALU.max, ALU.add))
                for u in range(QUAD):
                    last = nc.vector.bn_stats(stats[:, 6 * u:6 * u + 6], s[:, u * D:(u + 1) * D])
                step(last)
                for u in range(QUAD):
                    last = nc.vector.bn_aggr(mv3[:, u, :], stats[:, 6 * u:6 * u + 6])
                last.then_inc(var1_ready, 1)

            def diff_norm(m):
                dve.wait_ge(std1_ready, m + 1)
                step(nc.vector.reciprocal(rstd[:, 0:QUAD], std[:, 0:QUAD]))
                for u in range(QUAD):
                    last = ts(h3d[:, m * QUAD + u, :], diff_quad(m)[:, u * D:(u + 1) * D], mv3[:, u, 0:1],
                              rstd[:, u:u + 1], ALU.subtract, ALU.mult)
                last.then_inc(h2_ready, 1)
                dve.wait_ge(h2_ready, m + 1)

            def b4_parts(m):
                dve.wait_ge(b4_done, m + 1)
                step(nc.vector.tensor_copy(parts[1][:, m, 0, :], bank[6 + m % 2][:, :]))
                tt(parts[1][:, m, 1, :], bank[6 + m % 2][:, :], parts[1][:, m, 0, :], ALU.subtract)\
                    .then_inc(parts_ready, 1)

            for t in range(T):
                diff_add(t)
                if t >= QUAD and t % QUAD == 0:
                    diff_norm(t // QUAD - 1)
                if t % QUAD == QUAD - 1:
                    diff_finish(t // QUAD)
                    if t >= 2 * QUAD:
                        b4_parts(t // QUAD - 2)
            b4_parts(QUADS - 2)
            diff_norm(QUADS - 1)
            b4_parts(QUADS - 1)
            nc.vector.reduce_max(small[:, 8:9], deg[:, :], AX.X).then_inc(deg_max, 1)
            dve.wait_ge(pool_reduced, 1)
            step(ts(small[:, 10:11], small[:, 9:10], 4.0, 4.0, ALU.mult, ALU.add))
            step(ts(GROW.bitcast(i32), small[:, 10:11].bitcast(i32), EXPONENT_BITS, None, ALU.bitwise_and))
            step(nc.vector.reciprocal(INV_GROW, GROW))
            for k in (3, 2, 1):
                step(tt(S_K[k], S_K[k + 1], INV_GROW, ALU.mult))
            step(ts(EV, INV_GROW, 2.0, None, ALU.mult))
            step(stt(SUB, INV_GROW, -1.0, INV_GROW, ALU.mult, ALU.mult))
            step(nc.vector.reciprocal(EV0, S_K[1]))
            step(nc.vector.reciprocal(SUB0, S_K[2]))
            step(ts(SUB0, SUB0, -1.0, None, ALU.mult))
            for k in (3, 2, 1):
                step(ts(th_scaled[:, (3 - k) * D:(4 - k) * D], th[:, k * D:(k + 1) * D], S_K[k + 1], 0.5,
                        ALU.mult, ALU.mult))
            step(tt(th[:, 0:D], th[:, 0:D], ident[:, :], ALU.add))
            ts(th_scaled[:, 3 * D:4 * D], th[:, 0:D], S_K[1], None, ALU.mult).then_inc(theta_ready, 1)

            for q in range(ORDERS):
                k = ORDERS - 2 - q
                dst = parts[q % 2]
                for c in range(QUADS):
                    n = q * QUADS + c
                    back = bank[2 + n % 2][:, :]
                    if k >= 0 and k <= 2:
                        step(tt(old_b, dst[:, c, 0, :], dst[:, c, 1, :], ALU.add))
                    if k < 0:
                        step(tt(old_b, parts[1][:, c, 0, :], parts[1][:, c, 1, :], ALU.add))
                    dve.wait_ge(back_done, n + 1)
                    if k == 3:
                        nc.vector.tensor_copy(new_b, back).then_inc(back_read, 1)
                    else:
                        minus = SUB if k >= 1 else SUB0 if k == 0 else 1.0
                        stt(new_b, old_b, minus, back, ALU.mult, ALU.add).then_inc(back_read, 1)
                    dve.wait_ge(back_read, n + 1)
                    if k <= 0:
                        layer_norm(lambda t: new_b[:, t * D:(t + 1) * D], QUAD, var2_ready)
                        r = (q - ORDERS + 2) * QUADS + c
                        dve.wait_ge(std2_ready, r + 1)
                        step(nc.vector.reciprocal(rstd[:, 0:QUAD], std[:, 0:QUAD]))
                        if k < 0 and c >= 2:
                            dve.wait_ge(out_stored[c % 2], 16 * (c // 2))
                        dst_rows = new_b if k == 0 else out_slot(c)
                        for t in range(QUAD):
                            one = ts(dst_rows[:, t * D:(t + 1) * D], new_b[:, t * D:(t + 1) * D], mv3[:, t, 0:1],
                                     rstd[:, t:t + 1], ALU.subtract, ALU.mult)
                            if k == 0 or t < QUAD - 1:
                                step(one)
                        if k < 0:
                            one.then_inc(out_ready, 1)
                            continue
                    step(nc.vector.tensor_copy(dst[:, c, 0, :], new_b))
                    tt(dst[:, c, 1, :], new_b, dst[:, c, 0, :], ALU.subtract).then_inc(parts_ready, 1)
                    dve.wait_ge(parts_ready, (q + 1) * QUADS + c + 1)

        @block.tensor
        def _(pe):
            mm = nc.tensor.matmul
            pe.wait_ge(weights_in[0], 16)
            pe.wait_ge(weights_in[1], 16)
            for e in range(2):
                last = mm(bank[6][:, 2 * e:2 * e + 2], w1_sb[:, e * P:(e + 1) * P], w23_sb[:, :], start=True, stop=True)
            last.then_inc(v_done, 1)
            pe.wait_ge(w2_wide_ready, 1)
            for e in range(2):
                last = mm(bank[7][:, e * P:(e + 1) * P], w1_sb[:, e * P:(e + 1) * P], w2_wide, start=True, stop=True)
            last.then_inc(v_done, 1)
            pe.wait_ge(v_ready, 1)
            pe.wait_ge(in2_in[0], 16)
            pe.wait_ge(in2_in[1], 16)
            for t in range(T):
                for e in range(2):
                    last = mm(bank[6][:, 64 + 2 * t:66 + 2 * t], in2[:, e, t * P:(t + 1) * P],
                              v_cols[:, 2 * e:2 * e + 2], start=(e == 0), stop=(e == 1))
            last.then_inc(f_cols_done, 1)
            pe.wait_ge(v_ready, 2)
            for c in range(QUADS):
                if c >= 4:
                    pe.wait_ge(f1_row_ready, c - 3)
                for e in range(2):
                    last = mm(bank[c % 4][:, :], v1_wide[:, e, :], in2[:, e, c * WIDE:(c + 1) * WIDE],
                              start=(e == 0), stop=(e == 1))
                last.then_inc(f1_row_done, 1)
            pe.wait_ge(squares_ready, 1)
            mm(bank[5][:, :], ones[:, :], squares[:, 0:WIDE], start=True, stop=True)
            mm(bank[4][:, 0:2 * D], ones[:, :], squares[:, WIDE:WIDE + 2 * D], start=True, stop=True)\
                .then_inc(norms_done, 1)
            pe.wait_ge(x_in, 16)
            for t in range(T):
                last = mm(bank[7][:, 0:D], ones[:, :], x3[:, t, 0:D], start=(t == 0), stop=(t == T - 1))
            last.then_inc(xsum_done, 1)

            pe.wait_ge(f1_row_ready, QUADS)
            pe.wait_ge(part_scale_var, 1)
            UNROLL = SLOTS

            def weigh(c, j, k):
                first = k == 0 and j is k
                pe.wait_ge(weight_ready, j + (c * T + 1))
                for t in range(SPAN_TILES):
                    x_tile = x3[:, bass.ds(j, 1), :].rearrange("p a d -> p (a d)")
                    last = mm(att_acc(c, t), weight[:, k % SLOTS, t * P:(t + 1) * P], x_tile,
                              start=(first and t % PER_BANK == 0), stop=False, skip_group_check=True)
                last.then_inc(weight_used, 1)

            for c in range(SPANS):
                if c >= 2:
                    pe.wait_ge(h1_ready, SPAN_TILES * (c - 1))
                for j in range(UNROLL):
                    weigh(c, j, j)
                with pe.Fori(1, T // UNROLL) as group:
                    for k in range(UNROLL):
                        weigh(c, group * UNROLL + k, k)

            pe.wait_ge(flag_ready, 1)
            with pe.If(pe.value_load(flag[0:1, 0:1], min_val=0, max_val=1)):
                for c in range(SPANS):
                    pe.wait_ge(diag_ready, c + 1)
                    for t in range(SPAN_TILES):
                        b, o = 4 + t // QUAD, t % QUAD * P
                        last = mm(bank[b][:, o:o + P], ones[:, :], diag[:, t, :], start=True, stop=True)
                    last.then_inc(f1_spread, 1)
                    for j0, count in ((0, 1), (1, T - 1)):
                        with pe.Fori(j0, j0 + count) as j:
                            pe.wait_ge(careful_ready, c * T + j + 2)
                            for t in range(SPAN_TILES):
                                last = mm(att_acc(0, t), careful_weight[:, t * P:(t + 1) * P],
                                          x3[:, bass.ds(j, 1), :].rearrange("p a d -> p (a d)"),
                                          start=(j0 == 0 and t % PER_BANK == 0), stop=False, skip_group_check=True)
                            last.then_inc(careful_multiplied, 1)
                pe.wait_ge(careful_done, SPANS)

            def turn(m, b):
                for t in range(QUAD):
                    last = nc.tensor.transpose(bank[b][:, t * D:(t + 1) * D], h3d[:, m * QUAD + t, :], ident[:, :])
                return last

            def project(m):
                pe.wait_ge(turn_copied, m + 1)
                if m >= 2:
                    pe.wait_ge(g_low_ready, m - 1)
                for t in range(QUAD):
                    o = m % 2 * WIDE + t * P
                    last = mm(bank[4 + m % 2][:, t * D:(t + 1) * D], tmp[:, o:o + P], wt_sb[:, :], start=True, stop=True)
                last.then_inc(g_done, 1)

            pe.wait_ge(h1_ready, T)
            for m in range(QUADS):
                if m >= 2:
                    pe.wait_ge(turn_copied, m - 1)
                turn(m, m % 2).then_inc(turn_done, 1)
                if m >= 1:
                    project(m - 1)
            project(QUADS - 1)

            def turn_h2(m):
                pe.wait_ge(h2_ready, m + 1)
                if m >= 2:
                    pe.wait_ge(h2t_copied, m - 1)
                turn(m, 4 + m % 2).then_inc(h2t_done, 1)

            def start_b4(m):
                pe.wait_ge(h2t_copied, m + 1)
                if m >= 2:
                    pe.wait_ge(parts_ready, m - 1)
                for t in range(QUAD):
                    o = (m * QUAD + t) * P
                    last = mm(bank[6 + m % 2][:, t * D:(t + 1) * D], h2t[:, o:o + P], th[:, (ORDERS - 1) * D:],
                              start=True, stop=True)
                last.then_inc(b4_done, 1)

            for t in range(T):
                if t >= 4:
                    pe.wait_ge(diff_read, t - 3)
                for j in range(T):
                    if t == 0 and j % QUAD == 0:
                        pe.wait_ge(g_low_ready, j // QUAD + 1)
                    last = mm(bank[t % 4][:, 0:GW], adj3[:, j, t * P:(t + 1) * P], gparts[:, j, :],
                              start=(j == 0), stop=(j == T - 1))
                last.then_inc(diff_done, 1)
                if t >= 6 and t % QUAD == 2:
                    turn_h2(t // QUAD - 1)
                if t >= 7 and t % QUAD == 3:
                    start_b4(t // QUAD - 1)

            def turn_back(n):
                pe.wait_ge(acc_copied, n + 1)
                if n >= 2:
                    pe.wait_ge(back_read, n - 1)
                for t in range(QUAD):
                    last = nc.tensor.transpose(bank[2 + n % 2][:, t * D:(t + 1) * D],
                                               turned_slot(n)[:, t * P:(t + 1) * P], ident[:, :])
                last.then_inc(back_done, 1)

            for q in range(ORDERS):
                src = parts[(q + 1) % 2]
                plain = q == ORDERS - 1
                for c in range(QUADS):
                    n = q * QUADS + c
                    if n < 2:
                        pe.wait_ge(diff_read, T - QUAD + 1 + n)
                    else:
                        pe.wait_ge(acc_copied, n - 1)
                    for j in range(T):
                        if n == 0 and j == T - 3 * QUAD:
                            turn_h2(QUADS - 1)
                        if n == 0 and j == T - 2 * QUAD:
                            start_b4(QUADS - 1)
                        if c == 0 and j % QUAD == 0:
                            pe.wait_ge(parts_ready, q * QUADS + j // QUAD + 1)
                        for part in range(2):
                            last = mm(bank[n % 2][:, :], src[:, j // QUAD, part, j % QUAD * P:(j % QUAD + 1) * P],
                                      adj3[:, j, c * WIDE:(c + 1) * WIDE], start=(j == 0 and part == 0),
                                      stop=(plain and j == T - 1 and part == 1))
                        if j == 3 and c >= 1:
                            turn_back(n - 1)
                    if not plain:
                        if n == 0:
                            pe.wait_ge(theta_ready, 1)
                        last = mm(bank[n % 2][:, :], th_scaled[:, q * D:(q + 1) * D], h2t[:, c * WIDE:(c + 1) * WIDE],
                                  start=False, stop=True)
                    last.then_inc(acc_done, 1)
                turn_back(q * QUADS + QUADS - 1)


_SHAPES = dict(n=4096, tiles=32, p=128, spans=4, loads=16, pair=2, span=1024)


def kernel(x, adj, L0_gnn_inlayer2, L0_gnn_W1, L0_gnn_w2, L0_gnn_b2, L0_gnn_w3, L0_gnn_b3, L1_gnn_t, L1_gnn_alpha,
           L1_gnn_W, L1_gnn_b, L2_gnn_theta):
    import numpy as _np
    import concourse.bacc as _bacc
    from concourse import mybir as _mybir
    from concourse.bass_utils import run_bass_kernel_spmd as _run

    s = _SHAPES
    host = lambda a: _np.asarray(a)
    adj = host(adj)
    blocks = adj.T.reshape(s["loads"], s["pair"], s["p"], s["spans"], s["span"]).transpose(3, 0, 2, 1, 4)
    nodes = host(x).reshape(s["tiles"], s["p"], -1).transpose(1, 0, 2)
    in2_t = host(L0_gnn_inlayer2).T.reshape(2, s["p"], s["n"]).transpose(1, 0, 2)
    row = _np.concatenate([host(L0_gnn_b2).reshape(1), host(L0_gnn_b3).reshape(1), host(L1_gnn_alpha).reshape(1),
                           host(L1_gnn_b)])
    arrays = {
        "adj_blocks": blocks,
        "x_nodes": nodes,
        "in2_t": in2_t,
        "w1": host(L0_gnn_W1),
        "w23": _np.stack([host(L0_gnn_w2), host(L0_gnn_w3)], axis=1),
        "wt": host(L1_gnn_W).T,
        "theta": host(L2_gnn_theta).transpose(1, 0, 2),
        "row_params": _np.broadcast_to(row, (s["p"], row.shape[0])),
    }
    arrays = {k: _np.ascontiguousarray(v) for k, v in arrays.items()}
    nc = _bacc.Bacc("TRN2", target_bir_lowering=False, num_devices=1)
    args = [nc.dram_tensor(k, v.shape, _mybir.dt.from_np(v.dtype), kind="ExternalInput").ap() for k, v in arrays.items()]
    out = nc.dram_tensor("out", (s["n"], s["p"]), _mybir.dt.float32, kind="ExternalOutput").ap()
    gnn_kernel(nc, *args, out)
    return _run(nc, [arrays], core_ids=[0]).results[0]["out"]
```

```python
from contextlib import ExitStack

import numpy as np

import concourse.bass as bass
from concourse import mybir


def gnn_kernel(nc, adj_blocks, x_nodes, in2_t, w1, w32, wt, theta, row_params, out):
    fp32 = mybir.dt.float32
    fp16 = mybir.dt.float16
    fp8 = mybir.dt.float8e4
    i32 = mybir.dt.int32
    ALU = mybir.AluOpType
    ACT = mybir.ActivationFunctionType
    AX = mybir.AxisListType
    RMAX = bass.bass_isa.ReduceOp.max

    N = 4096
    D = 128
    P = 128
    T = N // P
    ORDERS = theta.shape[1]
    EPS = 1e-5
    SLOPE = 0.01
    TAU = 0.5
    COEFF = [2.0 / ORDERS * float(np.exp(-TAU * np.cos(np.pi * (k + 0.5) / ORDERS))) for k in range(ORDERS)]
    EXPONENT_BITS = 0x7F800000
    PART_TOP = 2.0 ** 15
    TINY = 1e-30

    PAIRS = 8
    LOGIT_LIMIT = 32.0
    LOW_LIMIT = 4000.0

    SPAN = 1024
    SPANS = N // SPAN
    SPAN_TILES = SPAN // P
    LOAD_TILES = 2
    LOADS = SPANS * T // LOAD_TILES
    LOADS_PER_SPAN = T // LOAD_TILES
    SLOTS = 4
    ADJ_SEMS = 8
    DX = D + 1
    PER_BANK = 3
    SPAN_BANKS = -(-SPAN_TILES // PER_BANK)
    QUAD = 4
    QUADS = T // QUAD
    WIDE = QUAD * D
    GW = 2 * D + 1

    with ExitStack() as ctx:
        def sb(name, shape, dt=fp32):
            return ctx.enter_context(nc.sbuf_tensor(name, shape, dt))

        def sem(name):
            return ctx.enter_context(nc.semaphore(name))

        adj8 = sb("adj8", [P, T * N], fp8)
        adj3 = adj8[:, :].rearrange("p (t n) -> p t n", t=T)
        in2 = adj8[:, (T - 8) * N:].bitcast(fp32).rearrange("p (c e n) -> p c e n", c=SPANS, e=2)
        xh = sb("xh", [P, T * DX])
        x3 = xh[:, :].rearrange("p (t d) -> p t d", t=T)
        h2t = xh[:, 0:N]
        h = sb("h", [P, N])
        h3d = h[:, :].rearrange("p (t d) -> p t d", t=T)
        G_SPACE = T * GW // 2
        work = sb("work", [P, G_SPACE + N])
        expo = work[:, 0:SLOTS * SPAN].rearrange("p (s n) -> p s n", s=SLOTS)
        weight = work[:, SLOTS * SPAN:2 * SLOTS * SPAN].rearrange("p (s n) -> p s n", s=SLOTS)
        gparts = work[:, 0:G_SPACE].bitcast(fp16).rearrange("p (t w) -> p t w", t=T)
        g_own = work[:, G_SPACE:G_SPACE + N].rearrange("p (t d) -> p t d", t=T)
        parts = [work[:, base:base + N].bitcast(fp16).rearrange("p (t q d) -> p t q d", t=T, q=2)
                 for base in (0, G_SPACE)]
        tmp = sb("tmp", [P, QUAD * DX + 2 * WIDE])
        xr = tmp[:, 0:SPAN_TILES * D].rearrange("p (t d) -> p t d", t=SPAN_TILES)
        x_halves = tmp[:, 1152:1152 + 2 * D].rearrange("p (t d) -> p t d", t=2)
        w32_sb = tmp[:, 1408:1408 + P]
        v_wide = tmp[:, 1024:1024 + 2 * P].rearrange("p (e n) -> p e n", e=2)
        squares = tmp[:, 0:(ORDERS + 1) * D]
        w1_sb = sb("w1_sb", [P, 2 * P])
        wt_sb = sb("wt_sb", [P, D])
        th = sb("th", [P, ORDERS * D])
        th_scaled = sb("th_scaled", [P, (ORDERS - 1) * D])
        rows = sb("rows", [P, 2 + D])
        b32_col, alpha_col, bias_row = rows[:, 0:1], rows[:, 1:2], rows[:, 2:2 + D]
        ident = sb("ident", [P, P])
        ones = sb("ones", [P, P])
        xsum = sb("xsum", [P, D])
        f1_cols = sb("f1_cols", [P, T])
        f2_cols = sb("f2_cols", [P, T])
        q_cols = sb("q_cols", [P, T])
        low_cols = sb("low_cols", [P, T])
        eps_col = sb("eps_col", [P, 1])
        isolated = sb("isolated", [P, SPAN_TILES])
        inv_isolated = sb("inv_isolated", [P, SPAN_TILES])
        denom = sb("denom", [P, SPAN_TILES])
        inv_denom = sb("inv_denom", [P, SPAN_TILES])
        stats = sb("stats", [P, 6 * SPAN_TILES])
        inv_deg = sb("inv_deg", [P, QUAD])
        no_deg = sb("no_deg", [P, QUAD])
        mv = sb("mv", [P, 2 * SPAN_TILES])
        mv3 = mv[:, :].rearrange("p (t k) -> p t k", k=2)
        std = sb("std", [P, SPAN_TILES])
        rstd = sb("rstd", [P, SPAN_TILES])
        deg = sb("deg", [P, T])
        limits = sb("limits", [P, 8])
        flag = sb("flag", [P, 1], i32)
        lift_cols = sb("lift_cols", [P, T])
        stage = work[:, 0:2 * LOAD_TILES * SPAN].rearrange("p (s t n) -> p s t n", s=2, t=LOAD_TILES)
        diag = work[:, 4096:4096 + SPAN].rearrange("p (t n) -> p t n", t=SPAN_TILES)
        run_max = work[:, 4096:4096 + SPAN]
        row_max = work[:, 5120:5120 + SPAN]
        exp_up, exp_low = run_max, row_max
        careful_weight = work[:, 6144:6144 + SPAN]
        up_row = work[:, 7168:7168 + SPAN]
        small = sb("small", [P, 16])
        scales = sb("scales", [P, 16])
        S_G, INV_SG, ONE_MINUS_A, S4, GROW, INV_GROW = [scales[:, n:n + 1] for n in range(6)]
        OWN = scales[:, 13:14]
        EV, SUB, EV0, SUB0 = [scales[:, n:n + 1] for n in range(6, 10)]
        S_K = {4: S4, 3: scales[:, 10:11], 2: scales[:, 11:12], 1: scales[:, 12:13]}

        bank = [ctx.enter_context(nc.psum_tensor(f"bank{n}", [P, WIDE], fp32)) for n in range(8)]

        weights_in = [sem(f"weights_in{n}") for n in range(5)]
        in2_in = [sem(f"in2_in{c}") for c in range(SPANS)]
        x_in = [sem("x_in0"), sem("x_in1")]
        adj_in = [sem(f"adj_in{n}") for n in range(ADJ_SEMS)]
        xr_in = sem("xr_in")
        out_stored = [sem("out_stored0"), sem("out_stored1")]
        const_ready = sem("const_ready")
        pool_reduced = sem("pool_reduced")
        dve_step = sem("dve_step")
        x_step = sem("x_step")
        v_done = sem("v_done")
        v_ready = sem("v_ready")
        f_row_done = sem("f_row_done")
        f_turned = sem("f_turned")
        f1_completed = [sem(f"f1_completed{c}") for c in range(SPANS)]
        f_cols_ready = sem("f_cols_ready")
        f_row_ready = sem("f_row_ready")
        squares_ready = sem("squares_ready")
        norms_done = sem("norms_done")
        part_scale_var = sem("part_scale_var")
        part_scale_root = sem("part_scale_root")
        q_ready = sem("q_ready")
        limits_ready = sem("limits_ready")
        limits_reduced = sem("limits_reduced")
        flag_ready = sem("flag_ready")
        careful_x_in = sem("careful_x_in")
        careful_in = [sem("careful_in0"), sem("careful_in1")]
        careful_used = [sem("careful_used0"), sem("careful_used1")]
        careful_step = sem("careful_step")
        diag_ready = sem("diag_ready")
        f1_spread = sem("f1_spread")
        row_max_ready = sem("row_max_ready")
        rows_ready = sem("rows_ready")
        exps_ready = sem("exps_ready")
        careful_ready = sem("careful_ready")
        careful_multiplied = sem("careful_multiplied")
        careful_var = sem("careful_var")
        careful_std = sem("careful_std")
        careful_done = sem("careful_done")
        careful_zeroed = sem("careful_zeroed")
        expo_ready = sem("expo_ready")
        weight_ready = sem("weight_ready")
        weight_used = sem("weight_used")
        var_ready = sem("var_ready")
        std_ready = sem("std_ready")
        last_sums_read = sem("last_sums_read")
        h1_ready = sem("h1_ready")
        turn_done = sem("turn_done")
        turn_copied = sem("turn_copied")
        g_done = sem("g_done")
        g_copied = sem("g_copied")
        g_low_ready = sem("g_low_ready")
        diff_done = sem("diff_done")
        diff_low = sem("diff_low")
        diff_read = sem("diff_read")
        var1_ready = sem("var1_ready")
        std1_ready = sem("std1_ready")
        h2_ready = sem("h2_ready")
        h2t_done = sem("h2t_done")
        h2t_copied = sem("h2t_copied")
        b4_done = sem("b4_done")
        parts_ready = sem("parts_ready")
        deg_max = sem("deg_max")
        theta_ready = sem("theta_ready")
        acc_done = sem("acc_done")
        acc_low = sem("acc_low")
        acc_read = sem("acc_read")
        var2_ready = sem("var2_ready")
        std2_ready = sem("std2_ready")
        out_ready = sem("out_ready")

        block = ctx.enter_context(nc.Block())

        def adj_target(load):
            c, j = load // LOADS_PER_SPAN, load % LOADS_PER_SPAN * LOAD_TILES
            return adj3[:, j:j + LOAD_TILES, c * SPAN:(c + 1) * SPAN]

        def wait_adj(eng, load):
            eng.wait_ge(adj_in[load % ADJ_SEMS], 16 * (load // ADJ_SEMS + 1))

        def att_acc(c, t, cols=slice(0, DX)):
            b = SPAN_BANKS * (c % 2) + t // PER_BANK
            base = t % PER_BANK * DX
            return bank[b][:, base + cols.start:base + cols.stop]

        UNROLL = SLOTS
        X_PIECES = slice(0, UNROLL), slice(UNROLL, T)
        LIMITS_AT = 24
        STD_AT = 20

        def f_row_bank(q):
            return bank[(3, 4, 6)[q % 3]]

        def f_turn_bank(q):
            return bank[(5, 7)[q % 2]]

        EARLY = QUADS - SPAN_TILES // QUAD

        def turned_h1(m):
            if m < EARLY:
                base = G_SPACE + (EARLY + m % 2) * WIDE
                return work[:, base:base + WIDE]
            return tmp[:, m % 2 * WIDE:(m % 2 + 1) * WIDE]

        def g_bank(m):
            return bank[(7, 2)[m % 2]]

        def diff_bank(t):
            return bank[(0, 1, 3, 4)[t % QUAD]]

        def h2_bank(m):
            return bank[(2, 5)[m % 2]]

        def low_slot(t):
            return tmp[:, t % QUAD * DX:(t % QUAD + 1) * DX]

        def sums(n):
            return [bank[n % 2 * 2 + pair][:, :].rearrange("p (t q d) -> p t q d", t=2, q=2) for pair in range(2)]

        def low_sums(n, pair):
            base = n % 2 * WIDE + pair * 2 * D
            return h[:, base:base + 2 * D].rearrange("p (t d) -> p t d", t=2)

        def tile_groups(k, c):
            return ((0, 2), (2, 4)) if k < 0 and c == QUADS - 1 else ((0, 4),)

        def out_slot(c):
            return h[:, (2 + c % 2) * WIDE:(3 + c % 2) * WIDE]

        old_b = h[:, 4 * WIDE:5 * WIDE]
        new_b = h[:, 5 * WIDE:6 * WIDE]
        old_b3, new_b3 = [b.rearrange("p (t d) -> p t d", t=QUAD) for b in (old_b, new_b)]

        @block.sync
        def _(sp):
            sp.dma_start(w1_sb[:, :], w1).then_inc(weights_in[0], 16)
            for c in range(SPANS):
                sp.dma_start(in2[:, c, :, :], in2_t[:, c, :, :]).then_inc(in2_in[c], 16)
            for c in range(SPANS):
                chunk = slice(c * SPAN, (c + 1) * SPAN)
                sp.wait_ge(f_turned, 2 * (c + 1))
                sp.dma_start(h[0:1, chunk], h[1:2, chunk]).then_inc(f1_completed[c], 16)
                if c < 2:
                    sp.dma_start(x3[:, X_PIECES[c], 0:D], x_nodes[:, X_PIECES[c], :]).then_inc(x_in[c], 16)
            sp.dma_start(wt_sb[:, :], wt).then_inc(weights_in[3], 16)
            sp.dma_start(th[:, :], theta.rearrange("p k d -> p (k d)")).then_inc(weights_in[4], 16)

            def load_residual(c):
                if c >= 1:
                    sp.wait_ge(h1_ready, SPAN_TILES * c)
                else:
                    sp.wait_ge(norms_done, 1)
                sp.dma_start(xr, x_nodes[:, c * SPAN_TILES:(c + 1) * SPAN_TILES, :]).then_inc(xr_in, 16)

            for c in range(SPANS):
                load_residual(c)

            sp.wait_ge(flag_ready, 1)
            with sp.If(sp.value_load(flag[0:1, 0:1], min_val=0, max_val=1)):
                sp.wait_ge(weight_used, SPANS * T)
                sp.wait_ge(xr_in, 16 * SPANS)
                for c in range(SPANS):
                    if c >= 1:
                        sp.wait_ge(careful_done, c)
                    sp.dma_start(xr, x_nodes[:, bass.ds(c * SPAN_TILES, SPAN_TILES), :]).then_inc(careful_x_in, 16)
                    for sweep in range(2):
                        if sweep == 1:
                            for s in range(2):
                                sp.wait_ge(careful_used[s], (c + 1) * PAIRS + 1)
                        with sp.Fori(0, PAIRS) as pair:
                            for s in range(2):
                                source = sp.snap(pair * 2 + s)
                                if sweep == 0:
                                    sp.wait_ge(careful_used[s], c * PAIRS + pair + 1)
                                else:
                                    sp.wait_ge(careful_ready, c * T + pair * 2 * LOAD_TILES + 1)
                                sp.dma_start(stage[:, s, :, :], adj_blocks[c, source, :, :, :])\
                                    .then_inc(careful_in[s], 16)
            out_tiles = out.rearrange("(t p) d -> p t d", p=P)
            stored = [0, 0]
            for c in range(QUADS):
                for a, b in tile_groups(-1, c):
                    sp.wait_ge(out_ready, sum(stored) + 1)
                    if a > 0:
                        sp.wait_ge(out_stored[c % 2], 16 * stored[c % 2])
                    stored[c % 2] += 1
                    sp.dma_start(out_tiles[:, c * QUAD + a:c * QUAD + b, :],
                                 out_slot(c)[:, a * D:b * D].rearrange("p (t d) -> p t d", t=b - a))\
                        .then_inc(out_stored[c % 2], 16)
            for s in range(2):
                sp.wait_ge(out_stored[s], 16 * stored[s])

        @block.gpsimd
        def _(pool):
            nc.gpsimd.memset(ones[:, :], 1.0).then_inc(const_ready, 1)
            nc.gpsimd.memset(eps_col[:, :], EPS).then_inc(const_ready, 1)
            nc.gpsimd.memset(ident[:, :], 0.0).then_inc(const_ready, 1)
            pool.wait_ge(const_ready, 3)
            nc.gpsimd.affine_select(out=ident[:, :], in_=ident[:, :], compare_op=ALU.not_equal, fill=1.0,
                                    base=0, pattern=[[-1, P]], channel_multiplier=1).then_inc(const_ready, 1)
            nc.gpsimd.memset(x3[:, :, D:DX], 1.0).then_inc(const_ready, 1)

            pool.wait_ge(in2_in[SPANS - 1], 16)
            for load in range(LOADS):
                if load == LOADS_PER_SPAN - 4:
                    for piece in x_in:
                        pool.wait_ge(piece, 16)
                    pool.wait_ge(f_turned, QUADS)
                    nc.gpsimd.tensor_tensor(x_halves, x3[:, 0:2, 0:D], x3[:, 2:4, 0:D], ALU.add).then_inc(x_step, 1)
                    for t in range(4, T, 2):
                        pool.wait_ge(x_step, t // 2 - 1)
                        nc.gpsimd.tensor_tensor(x_halves, x_halves, x3[:, t:t + 2, 0:D], ALU.add).then_inc(x_step, 1)
                if load >= ADJ_SEMS:
                    wait_adj(pool, load - ADJ_SEMS)
                pool.dma_start(adj_target(load), adj_blocks[load // LOADS_PER_SPAN, load % LOADS_PER_SPAN, :, :, :])\
                    .then_inc(adj_in[load % ADJ_SEMS], 16)
                if load == LIMITS_AT:
                    pool.wait_ge(limits_ready, 1)
                    nc.gpsimd.partition_all_reduce(limits[:, 4:6], limits[:, 2:4], P, RMAX)\
                        .then_inc(limits_reduced, 1)
            pool.wait_ge(flag_ready, 1)
            with pool.If(pool.value_load(flag[0:1, 0:1], min_val=0, max_val=1)):
                for c in range(SPANS):
                    pool.wait_ge(careful_used[1], (c + 1) * PAIRS + 1)
                    nc.gpsimd.partition_all_reduce(row_max, run_max, P, RMAX).then_inc(row_max_ready, 1)
            pool.wait_ge(deg_max, 1)
            nc.gpsimd.partition_all_reduce(small[:, 9:10], small[:, 8:9], P, RMAX).then_inc(pool_reduced, 1)

        @block.scalar
        def _(act):
            act.dma_start(w32_sb, w32).then_inc(weights_in[1], 16)
            act.dma_start(rows[:, :], row_params).then_inc(weights_in[2], 16)

            act.wait_ge(v_done, 1)
            nc.scalar.copy(v_wide, bank[5][:, 0:2 * P].rearrange("p (e n) -> p e n", e=2)).then_inc(v_ready, 1)

            def exponential(n):
                c, j = n // T, n % T
                if n >= SLOTS:
                    act.wait_ge(weight_ready, n - SLOTS + 1)
                nc.scalar.activation(expo[:, n % SLOTS, :], h[:, c * SPAN:(c + 1) * SPAN], ACT.Exp,
                                     bias=f2_cols[:, j:j + 1], scale=1.0 - SLOPE).then_inc(expo_ready, 1)

            act.wait_ge(weights_in[2], 16)
            for q in range(QUADS):
                act.wait_ge(f_row_done, q + 1)
                nc.scalar.activation(h[:, q * WIDE:(q + 1) * WIDE], f_row_bank(q)[:, :], ACT.Identity,
                                     bias=b32_col).then_inc(f_row_ready, 1)
                if q == 3:
                    act.wait_ge(f_cols_ready, 1)
                    nc.scalar.activation(q_cols[:, 0:QUAD], f2_cols[:, 0:QUAD], ACT.Exp, scale=SLOPE)\
                        .then_inc(q_ready, 1)
                if q == 4:
                    act.wait_ge(f1_completed[0], 16)
                if q >= 4:
                    exponential(q - 4)
            act.wait_ge(f_cols_ready, QUADS)
            nc.scalar.activation(q_cols[:, QUAD:], f2_cols[:, QUAD:], ACT.Exp, scale=SLOPE).then_inc(q_ready, 1)

            for c in range(SPANS):
                if c >= 1:
                    act.wait_ge(f1_completed[c], 16)
                for j in range(T):
                    if c * T + j >= SLOTS:
                        exponential(c * T + j)
                    if c == 1 and j == STD_AT:
                        act.wait_ge(part_scale_var, 1)
                        nc.scalar.activation(small[:, 4:6], small[:, 2:4], ACT.Sqrt).then_inc(part_scale_root, 1)
                    if c >= 1 and j == STD_AT:
                        act.wait_ge(var_ready, c)
                        nc.scalar.activation(std[:, :], mv3[:, :, 1], ACT.Sqrt, bias=eps_col[:, :])\
                            .then_inc(std_ready, 1)

            act.wait_ge(flag_ready, 1)
            with act.If(act.value_load(flag[0:1, 0:1], min_val=0, max_val=1)):
                for c in range(SPANS):
                    act.wait_ge(rows_ready, c + 1)
                    with act.Fori(0, T) as j:
                        act.wait_ge(careful_ready, c * T + j + 1)
                        nc.scalar.activation(exp_up, up_row, ACT.Exp, bias=f2_cols[:, bass.ds(j, 1)])
                        nc.scalar.activation(exp_low, h[:, bass.ds(c * SPAN, SPAN)], ACT.Exp,
                                             bias=low_cols[:, bass.ds(j, 1)]).then_inc(exps_ready, 1)
                    if c < SPANS - 1:
                        act.wait_ge(careful_var, c + 1)
                        nc.scalar.activation(std[:, :], mv3[:, :, 1], ACT.Sqrt, bias=eps_col[:, :])\
                            .then_inc(careful_std, 1)

            def copy_turned(m):
                act.wait_ge(turn_done, m + 1)
                if m >= 2:
                    act.wait_ge(g_done, m - 1)
                nc.scalar.copy(turned_h1(m), bank[6][:, :]).then_inc(turn_copied, 1)

            copy_turned(0)
            for m in range(QUADS):
                if m + 1 != EARLY and m + 1 < QUADS:
                    copy_turned(m + 1)
                if m == EARLY - 2:
                    act.wait_ge(var_ready, SPANS)
                    nc.scalar.activation(std[:, :], mv3[:, :, 1], ACT.Sqrt, bias=eps_col[:, :]).then_inc(std_ready, 1)
                act.wait_ge(g_done, m + 1)
                quad = slice(m * QUAD, (m + 1) * QUAD)
                g_psum = g_bank(m)[:, :].rearrange("p (t d) -> p t d", t=QUAD)
                nc.scalar.mul(gparts[:, quad, 0:D], g_psum, S_G)
                nc.scalar.mul(g_own[:, quad, :], g_psum, OWN).then_inc(g_copied, 1)
                if m + 1 == EARLY:
                    copy_turned(m + 1)

            for t in range(T + 4):
                if t < T:
                    act.wait_ge(diff_done, t + 1)
                    if t >= 4:
                        act.wait_ge(diff_read, t - 3)
                    nc.scalar.copy(low_slot(t), diff_bank(t)[:, D:GW]).then_inc(diff_low, 1)
                if t >= QUAD and t % QUAD == 0:
                    act.wait_ge(var1_ready, t // QUAD)
                    nc.scalar.activation(std[:, 0:QUAD], mv3[:, 0:QUAD, 1], ACT.Sqrt, bias=eps_col[:, :])\
                        .then_inc(std1_ready, 1)
                if t >= 6 and t % QUAD == 2:
                    m = t // QUAD - 1
                    act.wait_ge(h2t_done, m + 1)
                    nc.scalar.copy(h2t[:, m * WIDE:(m + 1) * WIDE], h2_bank(m)[:, :]).then_inc(h2t_copied, 1)

            act.wait_ge(theta_ready, 1)
            rooted = 0
            for q in range(ORDERS):
                k = ORDERS - 2 - q
                for c in range(QUADS):
                    n = q * QUADS + c
                    scale = EV if k >= 1 else EV0 if k == 0 else 1.0
                    if n >= 2:
                        act.wait_ge(acc_read, n - 1)
                    for pair in range(2):
                        act.wait_ge(acc_done, 2 * n + pair + 1)
                        nc.scalar.mul(low_sums(n, pair), sums(n)[pair][:, :, 1, :], scale).then_inc(acc_low, 1)
                    if k <= 0:
                        for a, b in tile_groups(k, c):
                            rooted += 1
                            act.wait_ge(var2_ready, rooted)
                            nc.scalar.activation(std[:, a:b], mv3[:, a:b, 1], ACT.Sqrt, bias=eps_col[:, :])\
                                .then_inc(std2_ready, 1)

        @block.vector
        def _(dve):
            steps = [0]

            def step(ins):
                steps[0] += 1
                ins.then_inc(dve_step, 1)
                dve.wait_ge(dve_step, steps[0])

            tt, ts, stt = nc.vector.tensor_tensor, nc.vector.tensor_scalar, nc.vector.scalar_tensor_tensor

            def weigh(n):
                c, j = n // T, n % T
                if n in (0, QUAD):
                    dve.wait_ge(q_ready, n // QUAD + 1)
                if j % LOAD_TILES == 0:
                    wait_adj(dve, n // LOAD_TILES)
                dve.wait_ge(expo_ready, n + 1)
                if n >= SLOTS:
                    dve.wait_ge(weight_used, n - SLOTS + 1)
                stt(weight[:, n % SLOTS, :], expo[:, n % SLOTS, :], q_cols[:, j:j + 1],
                    adj3[:, j, c * SPAN:(c + 1) * SPAN], ALU.max, ALU.mult).then_inc(weight_ready, 1)

            FIRST = 2
            for q in range(QUADS):
                tiles = slice(q * QUAD, (q + 1) * QUAD)
                turned = f_turn_bank(q)[:, 0:2 * QUAD].rearrange("p (t k) -> p t k", k=2)
                if q >= QUADS - 1 - FIRST and q < QUADS - 1:
                    weigh(q - (QUADS - 1 - FIRST))
                dve.wait_ge(f_turned, q + 1)
                nc.vector.tensor_copy(f1_cols[:, tiles], turned[:, :, 1])
                nc.vector.tensor_copy(f2_cols[:, tiles], turned[:, :, 0]).then_inc(f_cols_ready, 1)
            dve.wait_ge(f_cols_ready, QUADS)

            def limits_steps():
                step(nc.vector.reduce_max(limits[:, 0:1], f1_cols[:, :], AX.X))
                step(nc.vector.reduce_max(limits[:, 1:2], f2_cols[:, :], AX.X))
                step(ts(low_cols[:, :], f2_cols[:, :], -1.0, None, ALU.mult))
                step(nc.vector.reduce_max(limits[:, 3:4], low_cols[:, :], AX.X))
                step(tt(limits[:, 0:1], limits[:, 0:1], limits[:, 1:2], ALU.max))
                step(ts(low_cols[:, :], f2_cols[:, :], SLOPE, None, ALU.mult))
                stt(limits[:, 2:3], limits[:, 3:4], LOGIT_LIMIT / LOW_LIMIT, limits[:, 0:1], ALU.mult, ALU.max)\
                    .then_inc(limits_ready, 1)

            def square_steps():
                dve.wait_ge(weights_in[3], 16)
                dve.wait_ge(weights_in[4], 16)
                tt(squares[:, 0:D], wt_sb[:, :], wt_sb[:, :], ALU.mult)
                for k in range(ORDERS):
                    last = ts(th[:, k * D:(k + 1) * D], th[:, k * D:(k + 1) * D], COEFF[k], None, ALU.mult)
                step(last)
                tt(squares[:, D:], th[:, :], th[:, :], ALU.mult).then_inc(squares_ready, 1)

            def norm_steps():
                dve.wait_ge(norms_done, 1)
                nc.vector.reduce_max(small[:, 0:1], bank[6][:, 0:D], AX.X)
                nc.vector.reduce_max(small[:, 6:7], bank[6][:, D:WIDE], AX.X)
                step(nc.vector.reduce_max(small[:, 7:8], bank[7][:, 0:2 * D], AX.X))
                step(tt(small[:, 1:2], small[:, 6:7], small[:, 7:8], ALU.max))
                step(ts(small[:, 0:2], small[:, 0:2], D / PART_TOP ** 2, TINY, ALU.mult, ALU.max))
                nc.vector.reciprocal(small[:, 2:4], small[:, 0:2]).then_inc(part_scale_var, 1)

            def part_scale_steps():
                dve.wait_ge(part_scale_root, 1)
                step(ts(small[:, 10:12].bitcast(i32), small[:, 4:6].bitcast(i32), EXPONENT_BITS, None,
                        ALU.bitwise_and))
                nc.vector.tensor_copy(S_G, small[:, 10:11])
                ts(ONE_MINUS_A, alpha_col, -1.0, 1.0, ALU.mult, ALU.add)
                step(nc.vector.tensor_copy(S4, small[:, 11:12]))
                nc.vector.reciprocal(INV_SG, S_G)
                tt(OWN, ONE_MINUS_A, S_G, ALU.mult)
                step(ts(th[:, (ORDERS - 1) * D:], th[:, (ORDERS - 1) * D:], S4, None, ALU.mult))

            def att_scalars(c, step=step):
                for b in range(SPAN_BANKS):
                    k = min(PER_BANK, SPAN_TILES - b * PER_BANK)
                    sums = bank[SPAN_BANKS * (c % 2) + b][:, 0:k * DX].rearrange("p (t w) -> p t w", w=DX)[:, :, D]
                    cols = slice(b * PER_BANK, b * PER_BANK + k)
                    step(ts(isolated[:, cols], sums, 0.0, None, ALU.is_equal))
                    step(stt(denom[:, cols], isolated[:, cols], float(N), sums, ALU.mult, ALU.add))
                step(nc.vector.reciprocal(inv_denom[:, :], denom[:, :]))
                step(tt(inv_isolated[:, :], inv_denom[:, :], isolated[:, :], ALU.mult))

            def att_add(c, tiles, step=step):
                for t in tiles:
                    last = stt(xr[:, t, :], att_acc(c, t, slice(0, D)), inv_denom[:, t:t + 1], xr[:, t, :],
                               ALU.mult, ALU.add)
                if c == SPANS - 1:
                    last.then_inc(last_sums_read, 1)
                    dve.wait_ge(last_sums_read, 1)
                else:
                    step(last)

            def att_add_mean(tiles, step=step):
                for t in tiles:
                    last = stt(xr[:, t, :], xsum[:, :], inv_isolated[:, t:t + 1], xr[:, t, :], ALU.mult, ALU.add)
                step(last)

            def att_stats(tiles, step=step):
                for t in tiles:
                    last = nc.vector.bn_stats(stats[:, 6 * t:6 * t + 6], xr[:, t, :])
                step(last)

            def att_aggregate(tiles):
                for t in tiles:
                    last = nc.vector.bn_aggr(mv3[:, t, :], stats[:, 6 * t:6 * t + 6])
                return last

            def att_rstd(c):
                dve.wait_ge(std_ready, c + 1)
                step(nc.vector.reciprocal(rstd[:, :], std[:, :]))

            def att_norm(c, t):
                ts(h3d[:, c * SPAN_TILES + t, :], xr[:, t, :], mv3[:, t, 0:1], rstd[:, t:t + 1],
                   ALU.subtract, ALU.mult).then_inc(h1_ready, 1)

            for c in range(SPANS):
                for j in range(T):
                    n = c * T + j
                    if n >= FIRST:
                        weigh(n)
                    if n == 8:
                        limits_steps()
                    if n == 12:
                        square_steps()
                    if n == T + 10:
                        norm_steps()
                    if n == T + STD_AT + 3:
                        part_scale_steps()
                    if n == 2 * T:
                        dve.wait_ge(limits_reduced, 1)
                        ts(flag[:, :], limits[:, 4:5], LOGIT_LIMIT, None, ALU.is_gt).then_inc(flag_ready, 1)
                    if c >= 1:
                        if j == 3:
                            dve.wait_ge(weight_used, c * T)
                            att_scalars(c - 1)
                            if c == 1:
                                dve.wait_ge(norms_done, 1)
                                step(nc.vector.tensor_copy(xsum[:, :], bank[7][:, 2 * D:3 * D]))
                            dve.wait_ge(xr_in, 16 * c)
                        if j in (4, 8, 12, 16):
                            tiles = range(j // 2 - 2, j // 2)
                            att_add(c - 1, tiles)
                            att_add_mean(tiles)
                            att_stats(tiles)
                            last = att_aggregate(tiles)
                            if j == 16:
                                last.then_inc(var_ready, 1)
                        if j == STD_AT + 2:
                            att_rstd(c - 1)
                        if j >= T - SPAN_TILES:
                            att_norm(c - 1, j - (T - SPAN_TILES))
            dve.wait_ge(weight_used, SPANS * T)

            dve.wait_ge(flag_ready, 1)
            with dve.If(dve.value_load(flag[0:1, 0:1], min_val=0, max_val=1)):
                taken = [0, 0]

                def cstep(ins):
                    taken[0] += 1
                    ins.then_inc(careful_step, 1)
                    dve.wait_ge(careful_step, taken[1] + taken[0])

                for m, opened in enumerate((careful_used[0], careful_used[1], careful_ready, careful_multiplied)):
                    piece = slice(m * T // 4, (m + 1) * T // 4)
                    ts(lift_cols[:, piece], f2_cols[:, piece], limits[:, 5:6], 1.0, ALU.add, ALU.add)\
                        .then_inc(opened, 1)
                    dve.wait_ge(opened, 1)
                MAX_STEPS, WEIGH_STEPS = PAIRS * 2 * (LOAD_TILES - 1), T
                CHUNK_STEPS = SPAN_TILES - 1 + 2 + MAX_STEPS + 5 + WEIGH_STEPS + 2 * SPAN_BANKS + 2 + 3 + 1
                for c in range(SPANS):
                    taken[:] = [0, c * CHUNK_STEPS]
                    if c >= 1:
                        dve.wait_ge(careful_done, c)
                    for t in range(SPAN_TILES):
                        one = ts(diag[:, t, :], ident[:, :], f1_cols[:, bass.ds(c * SPAN_TILES + t, 1)], None, ALU.mult)
                        if t < SPAN_TILES - 1:
                            cstep(one)
                    one.then_inc(diag_ready, 1)
                    dve.wait_ge(f1_spread, c + 1)
                    f1_row = h[:, bass.ds(c * SPAN, SPAN)]
                    for half in range(2):
                        cstep(nc.vector.tensor_copy(h[:, bass.ds(c * SPAN + half * WIDE, WIDE)], bank[6 + half][:, :]))
                    dve.wait_ge(diag_ready, c + 1)
                    nc.vector.memset(run_max, 0.0).then_inc(careful_zeroed, 1)
                    dve.wait_ge(careful_zeroed, c + 1)
                    max_base = taken[1] + taken[0]
                    with dve.Fori(0, PAIRS) as pair:
                        for s in range(2):
                            dve.wait_ge(careful_in[s], (2 * c * PAIRS + pair + 1) * 16)
                            for u in range(LOAD_TILES):
                                j = pair * 2 * LOAD_TILES + s * LOAD_TILES + u
                                one = stt(run_max, stage[:, s, u, :], lift_cols[:, bass.ds(j, 1)], run_max,
                                          ALU.mult, ALU.max)
                                if u < LOAD_TILES - 1:
                                    one.then_inc(careful_step, 1)
                                    dve.wait_ge(careful_step, max_base + pair * 2 + s + 1)
                                else:
                                    one.then_inc(careful_used[s], 1)
                                    dve.wait_ge(careful_used[s], c * PAIRS + pair + 2)
                    taken[0] += MAX_STEPS
                    dve.wait_ge(row_max_ready, c + 1)
                    cstep(ts(row_max, row_max, limits[:, 5:6], 1.0, ALU.subtract, ALU.subtract))
                    cstep(tt(row_max, row_max, f1_row, ALU.add))
                    cstep(ts(run_max, row_max, SLOPE, None, ALU.mult))
                    cstep(tt(row_max, row_max, run_max, ALU.max))
                    cstep(tt(up_row, f1_row, row_max, ALU.subtract))
                    stt(f1_row, f1_row, SLOPE, row_max, ALU.mult, ALU.subtract).then_inc(rows_ready, 1)
                    dve.wait_ge(rows_ready, c + 1)
                    weigh_base = taken[1] + taken[0]
                    with dve.Fori(0, PAIRS) as pair:
                        for s in range(2):
                            dve.wait_ge(careful_in[s], ((2 * c + 1) * PAIRS + pair + 1) * 16)
                            for u in range(LOAD_TILES):
                                k = s * LOAD_TILES + u
                                dve.wait_ge(exps_ready, c * T + pair * 2 * LOAD_TILES + k + 1)
                                tt(exp_up, exp_up, exp_low, ALU.max).then_inc(careful_step, 1)
                                dve.wait_ge(careful_step, weigh_base + pair * 2 * LOAD_TILES + k + 1)
                                dve.wait_ge(careful_multiplied, c * T + pair * 2 * LOAD_TILES + k + 1)
                                stt(careful_weight, exp_up, 1.0, stage[:, s, u, :], ALU.min, ALU.mult)\
                                    .then_inc(careful_ready, 1)
                    taken[0] += WEIGH_STEPS
                    dve.wait_ge(careful_multiplied, c * T + T + 1)
                    dve.wait_ge(careful_x_in, c * 16 + 16)
                    if c == SPANS - 1:
                        continue
                    att_scalars(1, cstep)
                    tiles = range(SPAN_TILES)
                    att_add(1, tiles, cstep)
                    att_add_mean(tiles, cstep)
                    att_stats(tiles, cstep)
                    one = att_aggregate(tiles)
                    one.then_inc(careful_var, 1)
                    dve.wait_ge(careful_var, c + 1)
                    dve.wait_ge(careful_std, c + 1)
                    cstep(nc.vector.reciprocal(rstd[:, :], std[:, :]))
                    for t in range(SPAN_TILES):
                        one = ts(h3d[:, bass.ds(c * SPAN_TILES + t, 1), :], xr[:, t:t + 1, :], mv3[:, t, 0:1],
                                 rstd[:, t:t + 1], ALU.subtract, ALU.mult)
                    one.then_inc(careful_done, 1)
                    assert taken[0] == CHUNK_STEPS, taken[0]

            def g_low(m):
                quad = slice(m * QUAD, (m + 1) * QUAD)
                dve.wait_ge(g_copied, m + 1)
                g_psum = g_bank(m)[:, :].rearrange("p (t d) -> p t d", t=QUAD)
                stt(gparts[:, quad, D:2 * D], g_psum, S_G, gparts[:, quad, 0:D], ALU.mult, ALU.subtract)\
                    .then_inc(g_low_ready, 1)

            nc.vector.memset(gparts[:, :, 2 * D:GW], 1.0)
            att_scalars(SPANS - 1)
            dve.wait_ge(xr_in, 16 * SPANS)
            tiles = range(SPAN_TILES)
            att_add(SPANS - 1, tiles)
            g_low(0)
            att_add_mean(tiles)
            g_low(1)
            att_stats(tiles)
            g_low(2)
            att_aggregate(tiles).then_inc(var_ready, 1)
            g_low(3)
            att_rstd(SPANS - 1)
            for t in tiles:
                att_norm(SPANS - 1, t)
            for m in range(4, QUADS):
                g_low(m)

            def layer_norm(rows_in, tiles, ready):
                for t in tiles:
                    last = nc.vector.bn_stats(stats[:, 6 * t:6 * t + 6], rows_in(t))
                step(last)
                for t in tiles:
                    last = nc.vector.bn_aggr(mv3[:, t, :], stats[:, 6 * t:6 * t + 6])
                last.then_inc(ready, 1)

            def diff_quad(m):
                base = QUAD * DX + m % 2 * WIDE
                return tmp[:, base:base + WIDE]

            def diff_add(t):
                low = low_slot(t)
                dve.wait_ge(diff_low, t + 1)
                nc.vector.tensor_copy(deg[:, t:t + 1], low[:, D:DX])
                o = t % QUAD * D
                tt(diff_quad(t // QUAD)[:, o:o + D], diff_bank(t)[:, 0:D], low[:, 0:D], ALU.add).then_inc(diff_read, 1)

            def diff_finish(m):
                s, tiles = diff_quad(m), range(m * QUAD, (m + 1) * QUAD)
                dve.wait_ge(diff_read, (m + 1) * QUAD)
                step(ts(inv_deg[:, :], deg[:, m * QUAD:(m + 1) * QUAD], alpha_col, ONE_MINUS_A, ALU.mult, ALU.add))
                step(ts(no_deg[:, :], inv_deg[:, :], 0.0, None, ALU.is_equal))
                step(tt(inv_deg[:, :], inv_deg[:, :], no_deg[:, :], ALU.add))
                step(nc.vector.reciprocal(inv_deg[:, :], inv_deg[:, :]))
                step(ts(no_deg[:, :], no_deg[:, :], -1.0, 1.0, ALU.mult, ALU.add))
                step(stt(inv_deg[:, :], inv_deg[:, :], INV_SG, no_deg[:, :], ALU.mult, ALU.mult))
                own = g_own[:, m * QUAD:(m + 1) * QUAD, :].rearrange("p t d -> p (t d)")
                step(stt(s, s, alpha_col, own, ALU.mult, ALU.add))
                for u in range(QUAD):
                    last = stt(s[:, u * D:(u + 1) * D], s[:, u * D:(u + 1) * D], inv_deg[:, u:u + 1], bias_row,
                               ALU.mult, ALU.add)
                step(last)
                step(stt(s, s, 0.0, h[:, m * WIDE:(m + 1) * WIDE], ALU.max, ALU.add))
                for u in range(QUAD):
                    last = nc.vector.bn_stats(stats[:, 6 * u:6 * u + 6], s[:, u * D:(u + 1) * D])
                step(last)
                for u in range(QUAD):
                    last = nc.vector.bn_aggr(mv3[:, u, :], stats[:, 6 * u:6 * u + 6])
                last.then_inc(var1_ready, 1)

            def diff_norm(m):
                dve.wait_ge(std1_ready, m + 1)
                step(nc.vector.reciprocal(rstd[:, 0:QUAD], std[:, 0:QUAD]))
                for u in range(QUAD):
                    last = ts(h3d[:, m * QUAD + u, :], diff_quad(m)[:, u * D:(u + 1) * D], mv3[:, u, 0:1],
                              rstd[:, u:u + 1], ALU.subtract, ALU.mult)
                last.then_inc(h2_ready, 1)
                dve.wait_ge(h2_ready, m + 1)

            def b4_parts(m):
                dve.wait_ge(b4_done, m + 1)
                tiles = slice(m * QUAD, (m + 1) * QUAD)
                b = bank[6 + m % 2][:, :].rearrange("p (t d) -> p t d", t=QUAD)
                step(nc.vector.tensor_copy(parts[1][:, tiles, 0, :], b))
                tt(parts[1][:, tiles, 1, :], b, parts[1][:, tiles, 0, :], ALU.subtract).then_inc(parts_ready, 1)

            for t in range(T):
                diff_add(t)
                if t >= QUAD and t % QUAD == 0:
                    diff_norm(t // QUAD - 1)
                if t == T - 1:
                    dve.wait_ge(diff_read, T)
                    nc.vector.reduce_max(small[:, 8:9], deg[:, :], AX.X).then_inc(deg_max, 1)
                    b4_parts(QUADS - 2)
                if t % QUAD == QUAD - 1:
                    diff_finish(t // QUAD)
                    if QUAD < t < T - 1:
                        b4_parts(t // QUAD - 1)
            diff_norm(QUADS - 1)
            dve.wait_ge(pool_reduced, 1)
            step(ts(small[:, 10:11], small[:, 9:10], 4.0, 4.0, ALU.mult, ALU.add))
            step(ts(GROW.bitcast(i32), small[:, 10:11].bitcast(i32), EXPONENT_BITS, None, ALU.bitwise_and))
            step(nc.vector.reciprocal(INV_GROW, GROW))
            for k in (3, 2, 1):
                step(tt(S_K[k], S_K[k + 1], INV_GROW, ALU.mult))
            step(ts(EV, INV_GROW, 2.0, None, ALU.mult))
            step(stt(SUB, INV_GROW, -1.0, INV_GROW, ALU.mult, ALU.mult))
            step(nc.vector.reciprocal(EV0, S_K[1]))
            step(nc.vector.reciprocal(SUB0, S_K[2]))
            step(ts(SUB0, SUB0, -1.0, None, ALU.mult))
            for k in (3, 2, 1):
                step(ts(th_scaled[:, (3 - k) * D:(4 - k) * D], th[:, k * D:(k + 1) * D], S_K[k + 1], 0.5,
                        ALU.mult, ALU.mult))
            step(tt(th[:, 0:D], th[:, 0:D], ident[:, :], ALU.add))
            ts(th_scaled[:, 3 * D:4 * D], th[:, 0:D], S_K[1], None, ALU.mult).then_inc(theta_ready, 1)
            b4_parts(QUADS - 1)

            rooted = 0
            for q in range(ORDERS):
                k = ORDERS - 2 - q
                dst = parts[q % 2]
                for c in range(QUADS):
                    n = q * QUADS + c
                    tiles = slice(c * QUAD, (c + 1) * QUAD)
                    if k < 3:
                        old = parts[1] if k < 0 else dst
                        step(tt(old_b3, old[:, tiles, 0, :], old[:, tiles, 1, :], ALU.add))
                    scale = EV if k >= 1 else EV0 if k == 0 else 1.0
                    minus = SUB if k >= 1 else SUB0 if k == 0 else 1.0
                    for a, b in tile_groups(k, c):
                        cols = slice(a * D, b * D)
                        for pair in range(a // 2, b // 2):
                            dve.wait_ge(acc_low, 2 * n + pair + 1)
                            last = stt(new_b3[:, 2 * pair:2 * pair + 2, :], sums(n)[pair][:, :, 0, :], scale,
                                       low_sums(n, pair), ALU.mult, ALU.add)
                        if b == QUAD:
                            last.then_inc(acc_read, 1)
                            dve.wait_ge(acc_read, n + 1)
                        else:
                            step(last)
                        if k < 3:
                            step(stt(new_b[:, cols], old_b[:, cols], minus, new_b[:, cols], ALU.mult, ALU.add))
                        if k > 0:
                            continue
                        layer_norm(lambda t: new_b[:, t * D:(t + 1) * D], range(a, b), var2_ready)
                        rooted += 1
                        dve.wait_ge(std2_ready, rooted)
                        step(nc.vector.reciprocal(rstd[:, a:b], std[:, a:b]))
                        if k < 0 and c >= 2:
                            dve.wait_ge(out_stored[c % 2], 16 * (c // 2))
                        dst_rows = new_b if k == 0 else out_slot(c)
                        for t in range(a, b):
                            last = ts(dst_rows[:, t * D:(t + 1) * D], new_b[:, t * D:(t + 1) * D], mv3[:, t, 0:1],
                                      rstd[:, t:t + 1], ALU.subtract, ALU.mult)
                        if k < 0:
                            last.then_inc(out_ready, 1)
                        else:
                            step(last)
                    if k < 0:
                        continue
                    step(nc.vector.tensor_copy(dst[:, tiles, 0, :], new_b3))
                    tt(dst[:, tiles, 1, :], new_b3, dst[:, tiles, 0, :], ALU.subtract).then_inc(parts_ready, 1)
                    dve.wait_ge(parts_ready, (q + 1) * QUADS + c + 1)

        @block.tensor
        def _(pe):
            mm = nc.tensor.matmul
            pe.wait_ge(weights_in[0], 16)
            pe.wait_ge(weights_in[1], 16)
            for e in range(2):
                last = mm(bank[5][:, e * P:(e + 1) * P], w1_sb[:, e * P:(e + 1) * P], w32_sb, start=True, stop=True)
            last.then_inc(v_done, 1)

            def turn_f(q):
                pe.wait_ge(f_row_ready, q + 1)
                if q >= 2:
                    pe.wait_ge(f_cols_ready, q - 1)
                for t in range(QUAD):
                    o = (q * QUAD + t) * P
                    last = nc.tensor.transpose(f_turn_bank(q)[:, 2 * t:2 * t + 2], h[0:2, o:o + P], ident[0:2, 0:2])
                last.then_inc(f_turned, 1)

            pe.wait_ge(v_ready, 1)
            for q in range(QUADS):
                if q % 2 == 0:
                    pe.wait_ge(in2_in[q // 2], 16)
                if q >= 3:
                    pe.wait_ge(f_row_ready, q - 2)
                for e in range(2):
                    last = mm(f_row_bank(q)[:, :], v_wide[:, e, :],
                              in2[:, q // 2, e, q % 2 * WIDE:(q % 2 + 1) * WIDE], start=(e == 0), stop=(e == 1))
                last.then_inc(f_row_done, 1)
                if q == 0:
                    pe.wait_ge(const_ready, 5)
                else:
                    turn_f(q - 1)

            pe.wait_ge(x_in[0], 16)

            def weigh(c, j, k):
                first = k == 0 and j is k
                pe.wait_ge(weight_ready, j + (c * T + 1))
                for t in range(SPAN_TILES):
                    x_tile = x3[:, bass.ds(j, 1), :].rearrange("p a d -> p (a d)")
                    last = mm(att_acc(c, t), weight[:, k % SLOTS, t * P:(t + 1) * P], x_tile,
                              start=(first and t % PER_BANK == 0), stop=False, skip_group_check=True)
                last.then_inc(weight_used, 1)

            for c in range(SPANS):
                if c == 1:
                    pe.wait_ge(squares_ready, 1)
                    pe.wait_ge(x_step, T // 2 - 1)
                    mm(bank[6][:, :], ones[:, :], squares[:, 0:WIDE], start=True, stop=True)
                    mm(bank[7][:, 0:2 * D], ones[:, :], squares[:, WIDE:WIDE + 2 * D], start=True, stop=True)
                    for e in range(2):
                        last = mm(bank[7][:, 2 * D:3 * D], ones[:, :], x_halves[:, e, :], start=(e == 0), stop=(e == 1))
                    last.then_inc(norms_done, 1)
                if c >= 2:
                    pe.wait_ge(h1_ready, SPAN_TILES * (c - 1))
                for j in range(UNROLL):
                    weigh(c, j, j)
                    if c == 0 and j == 0:
                        turn_f(QUADS - 1)
                if c == 0:
                    pe.wait_ge(x_in[1], 16)
                with pe.Fori(1, T // UNROLL) as group:
                    for k in range(UNROLL):
                        weigh(c, group * UNROLL + k, k)

            pe.wait_ge(flag_ready, 1)
            with pe.If(pe.value_load(flag[0:1, 0:1], min_val=0, max_val=1)):
                for c in range(SPANS):
                    pe.wait_ge(diag_ready, c + 1)
                    for t in range(SPAN_TILES):
                        b, o = 6 + t // QUAD, t % QUAD * P
                        last = mm(bank[b][:, o:o + P], ones[:, :], diag[:, t, :], start=True, stop=True)
                    last.then_inc(f1_spread, 1)
                    for j0, count in ((0, 1), (1, T - 1)):
                        with pe.Fori(j0, j0 + count) as j:
                            pe.wait_ge(careful_ready, c * T + j + 2)
                            for t in range(SPAN_TILES):
                                last = mm(att_acc(1, t), careful_weight[:, t * P:(t + 1) * P],
                                          x3[:, bass.ds(j, 1), :].rearrange("p a d -> p (a d)"),
                                          start=(j0 == 0 and t % PER_BANK == 0), stop=False, skip_group_check=True)
                            last.then_inc(careful_multiplied, 1)
                pe.wait_ge(careful_done, SPANS - 1)

            def turn(m, b):
                for t in range(QUAD):
                    last = nc.tensor.transpose(b[:, t * D:(t + 1) * D], h3d[:, m * QUAD + t, :], ident[:, :])
                return last

            def turn_h1(m):
                pe.wait_ge(h1_ready, (m + 1) * QUAD)
                if m >= 1:
                    pe.wait_ge(turn_copied, m)
                turn(m, bank[6]).then_inc(turn_done, 1)

            def project(m):
                pe.wait_ge(turn_copied, m + 1)
                if m >= 2:
                    pe.wait_ge(g_low_ready, m - 1)
                for t in range(QUAD):
                    last = mm(g_bank(m)[:, t * D:(t + 1) * D], turned_h1(m)[:, t * P:(t + 1) * P], wt_sb[:, :],
                              start=True, stop=True)
                last.then_inc(g_done, 1)

            def turn_h2(m):
                pe.wait_ge(h2_ready, m + 1)
                if m >= 2:
                    pe.wait_ge(h2t_copied, m - 1)
                turn(m, h2_bank(m)).then_inc(h2t_done, 1)

            def start_b4(m):
                pe.wait_ge(h2t_copied, m + 1)
                if m >= 2:
                    pe.wait_ge(parts_ready, m - 1)
                for t in range(QUAD):
                    o = (m * QUAD + t) * P
                    last = mm(bank[6 + m % 2][:, t * D:(t + 1) * D], h2t[:, o:o + P], th[:, (ORDERS - 1) * D:],
                              start=True, stop=True)
                last.then_inc(b4_done, 1)

            def diffuse(t, sources):
                for j in sources:
                    last = mm(diff_bank(t)[:, 0:GW], adj3[:, j, t * P:(t + 1) * P], gparts[:, j, :],
                              start=(j == 0), stop=(j == T - 1))
                return last

            def diffuse_early(m):
                pe.wait_ge(g_low_ready, m + 1)
                for t in range(QUAD):
                    if m == 0 and t == 2:
                        pe.wait_ge(last_sums_read, 1)
                    diffuse(t, range(m * QUAD, (m + 1) * QUAD))

            turn_h1(0)
            for m in range(EARLY):
                if m + 1 < EARLY:
                    turn_h1(m + 1)
                project(m)
                if m >= 2:
                    diffuse_early(m - 2)
            for m in range(EARLY, QUADS):
                turn_h1(m)
            diffuse_early(EARLY - 2)
            for m in range(EARLY, QUADS):
                project(m)
            diffuse_early(EARLY - 1)
            for t in range(T):
                if t == 0:
                    pe.wait_ge(g_low_ready, QUADS)
                if t >= QUAD:
                    pe.wait_ge(diff_read, t - QUAD + 1)
                diffuse(t, range(EARLY * QUAD if t < QUAD else 0, T)).then_inc(diff_done, 1)
                if t >= 6 and t % QUAD == 2:
                    turn_h2(t // QUAD - 1)
                if t >= 7 and t % QUAD == 3:
                    start_b4(t // QUAD - 1)

            for q in range(ORDERS):
                src = parts[(q + 1) % 2]
                plain = q == ORDERS - 1
                for c in range(QUADS):
                    n = q * QUADS + c
                    if n < 2:
                        pe.wait_ge(diff_read, T - QUAD + 2 * (n + 1))
                    else:
                        pe.wait_ge(acc_read, n - 1)

                    def accumulate(u, sources):
                        t = c * QUAD + u
                        for j in sources:
                            if c == 0 and u == 0 and j % QUAD == 0 or j == T - QUAD and c == 0:
                                pe.wait_ge(parts_ready, q * QUADS + j // QUAD + 1)
                            last = mm(sums(n)[u // 2][:, u % 2, :, :].rearrange("p q d -> p (q d)"),
                                      adj3[:, j, t * P:(t + 1) * P],
                                      src[:, j, :, :].rearrange("p q d -> p (q d)"),
                                      start=(j == 0 and u % 2 == 0), stop=False, skip_group_check=True)
                        return last

                    def finish(u):
                        t = c * QUAD + u
                        if n == 0 and u == 0:
                            pe.wait_ge(theta_ready, 1)
                        return mm(sums(n)[u // 2][:, u % 2, 0, :], h2t[:, t * P:(t + 1) * P],
                                  th_scaled[:, q * D:(q + 1) * D], start=False, stop=False, skip_group_check=True)

                    split = T - QUAD if c == 0 else 0
                    for u in range(QUAD if c == 0 else 0):
                        if n == 0 and u == QUAD - 1:
                            turn_h2(QUADS - 1)
                            accumulate(u, range(split // 2))
                            start_b4(QUADS - 1)
                            accumulate(u, range(split // 2, split))
                        else:
                            accumulate(u, range(split))
                    for u in range(QUAD):
                        last = accumulate(u, range(split, T))
                        if not plain:
                            last = finish(u)
                        if u % 2 == 1:
                            last.then_inc(acc_done, 1)


_SHAPES = dict(n=4096, tiles=32, p=128, spans=4, loads=16, pair=2, span=1024)


def kernel(x, adj, L0_gnn_inlayer2, L0_gnn_W1, L0_gnn_w2, L0_gnn_b2, L0_gnn_w3, L0_gnn_b3, L1_gnn_t, L1_gnn_alpha,
           L1_gnn_W, L1_gnn_b, L2_gnn_theta):
    import numpy as _np
    import concourse.bacc as _bacc
    from concourse import mybir as _mybir
    from concourse.bass_utils import run_bass_kernel_spmd as _run

    s = _SHAPES
    host = lambda a: _np.asarray(a)
    adj = host(adj)
    blocks = adj.T.reshape(s["loads"], s["pair"], s["p"], s["spans"], s["span"]).transpose(3, 0, 2, 1, 4)
    nodes = host(x).reshape(s["tiles"], s["p"], -1).transpose(1, 0, 2)
    in2_t = host(L0_gnn_inlayer2).T.reshape(2, s["p"], s["spans"], s["span"]).transpose(1, 2, 0, 3)
    w2, w3 = host(L0_gnn_w2).reshape(-1, 1), host(L0_gnn_w3).reshape(-1, 1)
    b2, b3 = host(L0_gnn_b2).reshape(1, 1), host(L0_gnn_b3).reshape(1, 1)
    row = _np.concatenate([host(L1_gnn_alpha).reshape(1), host(L1_gnn_b)])
    arrays = {
        "adj_blocks": blocks,
        "x_nodes": nodes,
        "in2_t": in2_t,
        "w1": host(L0_gnn_W1),
        "w32": _np.concatenate([w3] + [w2] * (s["p"] - 1), axis=1),
        "wt": host(L1_gnn_W).T,
        "theta": host(L2_gnn_theta).transpose(1, 0, 2),
        "row_params": _np.concatenate([_np.concatenate([b3] + [b2] * (s["p"] - 1)),
                                       _np.broadcast_to(row, (s["p"], row.shape[0]))], axis=1),
    }
    arrays = {k: _np.ascontiguousarray(v) for k, v in arrays.items()}
    nc = _bacc.Bacc("TRN2", target_bir_lowering=False, num_devices=1)
    args = [nc.dram_tensor(k, v.shape, _mybir.dt.from_np(v.dtype), kind="ExternalInput").ap() for k, v in arrays.items()]
    out = nc.dram_tensor("out", (s["n"], s["p"]), _mybir.dt.float32, kind="ExternalOutput").ap()
    gnn_kernel(nc, *args, out)
    return _run(nc, [arrays], core_ids=[0]).results[0]["out"]
```
